# Optimizing a Trainium2 kernel written in Bass

```python
import numpy as np
import jax
import jax.numpy as jnp

def _softmax(x, axis=-1):
    return jax.nn.softmax(x, axis=axis)

def _gelu(x):
    return jax.nn.gelu(x, approximate=True)

def _silu(x):
    return jax.nn.silu(x)

def _sigmoid(x):
    return jax.nn.sigmoid(x)

def _layernorm(x, axis=-1, eps=1e-05):
    m = jnp.mean(x, axis=axis, keepdims=True)
    v = jnp.var(x, axis=axis, keepdims=True)
    return (x - m) / jnp.sqrt(v + eps)

def _scatter_add(tgt, idx, src, axis=0):
    return tgt.at[idx].add(src)

def _segment_sum(src, seg, n):
    return jax.ops.segment_sum(src, seg, n)
kernel_name = 'mk_seq_postln_d1_jaxref_r8_652717'

def setup_inputs(seed: int=0):
    np.random.seed(seed)
    _w = jnp.asarray

    def _L0_attn_setup():
        import jax, jax.numpy as jnp
        import numpy as np
        HID = 256
        H = 16
        QLR = 192
        KVLR = 64
        DN = 128
        DR = 64
        DV = 128
        DQ = DN + DR
        B = 2
        S = 256
        THETA = 10000.0
        EPS = 1e-06

        def rms_norm(x, w, eps=EPS):
            x32 = x.astype(jnp.float32)
            var = jnp.mean(x32 * x32, axis=-1, keepdims=True)
            return (w * (x32 * jax.lax.rsqrt(var + eps))).astype(x.dtype)

        def rotate_half(x):
            x1, x2 = jnp.split(x, 2, axis=-1)
            return jnp.concatenate((-x2, x1), axis=-1)

        def rope_tables(seq_len, dim, base=THETA):
            inv_freq = 1.0 / base ** (jnp.arange(0, dim, 2, dtype=jnp.float32) / dim)
            t = jnp.arange(seq_len, dtype=jnp.float32)
            freqs = jnp.outer(t, inv_freq)
            emb = jnp.concatenate((freqs, freqs), -1)
            return (jnp.cos(emb), jnp.sin(emb))
        key = jax.random.key(seed)
        ks = jax.random.split(key, 8)
        sd = lambda fan_in: 1.0 / np.sqrt(fan_in)
        return {'hidden_states': jax.random.normal(ks[0], (B, S, HID), jnp.float32), 'w_qa': jax.random.normal(ks[1], (QLR, HID), jnp.float32) * sd(HID), 'q_a_ln_w': jnp.ones((QLR,), jnp.float32), 'w_qb': jax.random.normal(ks[2], (H * DQ, QLR), jnp.float32) * sd(QLR), 'w_kva': jax.random.normal(ks[3], (KVLR + DR, HID), jnp.float32) * sd(HID), 'kv_a_ln_w': jnp.ones((KVLR,), jnp.float32), 'w_kvb': jax.random.normal(ks[4], (H * (DN + DV), KVLR), jnp.float32) * sd(KVLR), 'w_o': jax.random.normal(ks[5], (HID, H * DV), jnp.float32) * sd(H * DV)}
    _L0_attn_in = _L0_attn_setup()

    def _L0_ffn_setup():
        import jax, jax.numpy as jnp
        import numpy as np
        B, S, DIM = (2, 256, 256)
        E, K = (8, 2)
        H = DIM * 4 // 3
        key = jax.random.key(seed)
        ks = jax.random.split(key, 8)
        s = 0.02
        x = jax.random.normal(ks[0], (B, S, DIM), dtype=jnp.float32)
        sw1 = jax.random.normal(ks[1], (H, DIM), dtype=jnp.float32) * s
        sw2 = jax.random.normal(ks[2], (DIM, H), dtype=jnp.float32) * s
        sw3 = jax.random.normal(ks[3], (H, DIM), dtype=jnp.float32) * s
        ew1 = jax.random.normal(ks[4], (E, H, DIM), dtype=jnp.float32) * s
        ew2 = jax.random.normal(ks[5], (E, DIM, H), dtype=jnp.float32) * s
        ew3 = jax.random.normal(ks[6], (E, H, DIM), dtype=jnp.float32) * s
        wr = jax.random.normal(ks[7], (E, DIM), dtype=jnp.float32) * s
        return {'x': x, 'sw1': sw1, 'sw2': sw2, 'sw3': sw3, 'ew1': ew1, 'ew2': ew2, 'ew3': ew3, 'wr': wr}
    _L0_ffn_in = _L0_ffn_setup()
    _d = {'L0_attn_hidden_states': _L0_attn_in['hidden_states'], 'L0_attn_w_qa': _L0_attn_in['w_qa'], 'L0_attn_q_a_ln_w': _L0_attn_in['q_a_ln_w'], 'L0_attn_w_qb': _L0_attn_in['w_qb'], 'L0_attn_w_kva': _L0_attn_in['w_kva'], 'L0_attn_kv_a_ln_w': _L0_attn_in['kv_a_ln_w'], 'L0_attn_w_kvb': _L0_attn_in['w_kvb'], 'L0_attn_w_o': _L0_attn_in['w_o'], 'L0_ffn_sw1': _L0_ffn_in['sw1'], 'L0_ffn_sw2': _L0_ffn_in['sw2'], 'L0_ffn_sw3': _L0_ffn_in['sw3'], 'L0_ffn_ew1': _L0_ffn_in['ew1'], 'L0_ffn_ew2': _L0_ffn_in['ew2'], 'L0_ffn_ew3': _L0_ffn_in['ew3'], 'L0_ffn_wr': _L0_ffn_in['wr']}
    _x0 = _d['L0_attn_hidden_states']
    _d['L0_attn_hidden_states'] = jax.random.normal(jax.random.fold_in(jax.random.key(seed), 1), (16, 256, 256), dtype=_x0.dtype)
    del _x0
    return _d

def reference(L0_attn_hidden_states, L0_attn_w_qa, L0_attn_q_a_ln_w, L0_attn_w_qb, L0_attn_w_kva, L0_attn_kv_a_ln_w, L0_attn_w_kvb, L0_attn_w_o, L0_ffn_sw1, L0_ffn_sw2, L0_ffn_sw3, L0_ffn_ew1, L0_ffn_ew2, L0_ffn_ew3, L0_ffn_wr):

    def _L0_attn_ref(hidden_states, w_qa, q_a_ln_w, w_qb, w_kva, kv_a_ln_w, w_kvb, w_o):
        import jax, jax.numpy as jnp
        import numpy as np
        HID = 256
        H = 16
        QLR = 192
        KVLR = 64
        DN = 128
        DR = 64
        DV = 128
        DQ = DN + DR
        B = 2
        S = 256
        THETA = 10000.0
        EPS = 1e-06

        def rms_norm(x, w, eps=EPS):
            x32 = x.astype(jnp.float32)
            var = jnp.mean(x32 * x32, axis=-1, keepdims=True)
            return (w * (x32 * jax.lax.rsqrt(var + eps))).astype(x.dtype)

        def rotate_half(x):
            x1, x2 = jnp.split(x, 2, axis=-1)
            return jnp.concatenate((-x2, x1), axis=-1)

        def rope_tables(seq_len, dim, base=THETA):
            inv_freq = 1.0 / base ** (jnp.arange(0, dim, 2, dtype=jnp.float32) / dim)
            t = jnp.arange(seq_len, dtype=jnp.float32)
            freqs = jnp.outer(t, inv_freq)
            emb = jnp.concatenate((freqs, freqs), -1)
            return (jnp.cos(emb), jnp.sin(emb))
        b, s, _ = hidden_states.shape
        scale = DQ ** (-0.5)
        cos, sin = rope_tables(s, DR)
        cq = rms_norm(hidden_states @ w_qa.T, q_a_ln_w)
        q = (cq @ w_qb.T).reshape(b, s, H, DQ).transpose(0, 2, 1, 3)
        q_nope, q_pe = (q[..., :DN], q[..., DN:])
        q_pe = q_pe * cos + rotate_half(q_pe) * sin
        ckv = hidden_states @ w_kva.T
        k_pe = ckv[..., KVLR:].reshape(b, s, 1, DR).transpose(0, 2, 1, 3)
        k_pe = k_pe * cos + rotate_half(k_pe) * sin
        ckv_l = rms_norm(ckv[..., :KVLR], kv_a_ln_w)
        kv = (ckv_l @ w_kvb.T).reshape(b, s, H, DN + DV).transpose(0, 2, 1, 3)
        k_nope, v = (kv[..., :DN], kv[..., DN:])
        q_full = jnp.concatenate([q_nope, q_pe], axis=-1)
        k_full = jnp.concatenate([k_nope, jnp.broadcast_to(k_pe, (b, H, s, DR))], axis=-1)
        scores = jnp.einsum('bhqd,bhkd->bhqk', q_full, k_full) * scale
        causal = jnp.triu(jnp.ones((s, s), dtype=bool), k=1)
        scores = jnp.where(causal, -jnp.inf, scores)
        attn = jax.nn.softmax(scores.astype(jnp.float32), axis=-1).astype(q_full.dtype)
        out = jnp.einsum('bhqk,bhkd->bhqd', attn, v)
        out = out.transpose(0, 2, 1, 3).reshape(b, s, H * DV)
        return out @ w_o.T

    def _L0_ffn_ref(x, sw1, sw2, sw3, ew1, ew2, ew3, wr):
        import jax, jax.numpy as jnp
        import numpy as np
        B, S, DIM = (2, 256, 256)
        E, K = (8, 2)
        H = DIM * 4 // 3
        shared = jax.nn.silu(x @ sw1.T) * (x @ sw3.T) @ sw2.T
        logits = x @ wr.T
        probs = jax.nn.softmax(logits, axis=-1)
        top_p, top_i = jax.lax.top_k(probs, K)
        top_p = top_p / jnp.sum(top_p, axis=-1, keepdims=True)
        gates = jnp.sum(jax.nn.one_hot(top_i, E, dtype=x.dtype) * top_p[..., None], axis=-2)
        u = jnp.einsum('bsd,ehd->bseh', x, ew1)
        v = jnp.einsum('bsd,ehd->bseh', x, ew3)
        h = jax.nn.silu(u) * v
        eo = jnp.einsum('bseh,edh->bsed', h, ew2)
        return shared + jnp.einsum('bsed,bse->bsd', eo, gates)
    x = L0_attn_hidden_states
    x = _layernorm(x + _L0_attn_ref(x, L0_attn_w_qa, L0_attn_q_a_ln_w, L0_attn_w_qb, L0_attn_w_kva, L0_attn_kv_a_ln_w, L0_attn_w_kvb, L0_attn_w_o), axis=-1)
    x = _layernorm(x + _L0_ffn_ref(x, L0_ffn_sw1, L0_ffn_sw2, L0_ffn_sw3, L0_ffn_ew1, L0_ffn_ew2, L0_ffn_ew3, L0_ffn_wr), axis=-1)
    return x

_drawn_inputs = setup_inputs


def setup_inputs(seed=0):
    import zlib

    import numpy as np

    out = dict(_drawn_inputs(seed))
    spreads = {'L0_attn_q_a_ln_w': (1.0, 0.2), 'L0_attn_kv_a_ln_w': (1.0, 0.2)}
    factors = {'L0_ffn_sw1': 2.801,
     'L0_ffn_ew1': 4.124,
     'L0_ffn_ew2': 4.091,
     'L0_ffn_ew3': 4.079,
     'L0_ffn_wr': 4.699}
    for name, (base, spread) in spreads.items():
        noise = np.random.default_rng([zlib.crc32(name.encode()), seed]).standard_normal(out[name].shape)
        drawn = base * np.exp(spread * noise) if base else spread * noise
        out[name] = jnp.asarray(drawn.astype(out[name].dtype))
    for name, factor in factors.items():
        out[name] = (out[name] * factor).astype(out[name].dtype)
    return out
```

```python
from contextlib import ExitStack

import concourse.bass as bass
from concourse import mybir

F32 = mybir.dt.float32
F32R = mybir.dt.float32r
ALU = mybir.AluOpType
ACT = mybir.ActivationFunctionType
AX = mybir.AxisListType

P = 128
NB, S, D = 16, 256, 256
H, QL, KL = 16, 192, 64
DN, DR, DV = 128, 64, 128
DQ = DN + DR
NA = QL + KL + DR
SCALE = float(DQ) ** -0.5
RMS_EPS, LN_EPS = 1e-6, 1e-5
MASKED = -1e30
PAIRS = H // 2
TT = NB * S // P
BATCH_STEPS = PAIRS
BODY = 2 * BATCH_STEPS
LAG_QT, LAG_SC, LAG_SM, LAG_PV, LAG_WO = 2, 3, 4, 5, 6

E = 8
HF = 4 * D // 3
MT = [128, 128, HF - 256]
C = 512
NC = NB * S // C
W3_AT, W2_AT = 2 * HF, 4 * HF
PIECES = NC - 1
PIECE = -(-(W2_AT + 3 * D) // PIECES)
WCOLS = PIECE * PIECES


def build(nc, x, xT, waT, wqb, wqbT, wkvb, woT, aln, kvln, rope, wrT, wffn, x1_dram, out):
    with ExitStack() as top:
        names = {}

        def sb(stack, name, shape, dt=F32):
            return stack.enter_context(nc.sbuf_tensor(name, shape, dt))

        def bank(name):
            return top.enter_context(nc.psum_tensor(name, [P, 512], F32))

        def sem(name):
            if name not in names:
                names[name] = top.enter_context(nc.semaphore(name))
            return names[name]

        ident = sb(top, "ident", [P, P])
        held = sb(top, "held", [P, 16])
        held_in = sb(top, "held_in", [P, 1])
        wraw = sb(top, "wraw", [P, WCOLS])
        with ExitStack() as staging:
            wa_raw = sb(staging, "wa_raw", [P, 2, NA])
            wq_nope = sb(staging, "wq_nope", [P, H, QL])
            wk_nat = sb(staging, "wk_nat", [P, H, KL])
            wv_nat = sb(staging, "wv_nat", [P, H, KL])
            wo_t = sb(staging, "wo_t", [P, H, D])
            wq_pe = sb(staging, "wq_pe", [P, 2, H, DR])
        x1T_hi = sb(top, "x1T_hi", [P, 2, NB * S], F32R)
        x1T_lo = sb(top, "x1T_lo", [P, 2, NB * S], F32R)

        with ExitStack() as att:
            wa_hi = sb(att, "wa_hi", [P, 2, NA], F32R)
            wa_lo = sb(att, "wa_lo", [P, 2, NA], F32R)
            m_hi = sb(att, "m_hi", [P, 2, H, P], F32R)
            m_lo = sb(att, "m_lo", [P, 2, H, P], F32R)
            wvo_hi = sb(att, "wvo_hi", [P, PAIRS, D], F32R)
            wvo_lo = sb(att, "wvo_lo", [P, PAIRS, D], F32R)
            aln_c = sb(att, "aln_c", [P, 2])
            kvln2 = sb(att, "kvln2", [P, 1])
            kvln1 = sb(att, "kvln1", [P, 1])
            cos = sb(att, "cos", [P, 2, DR])
            sgn = sb(att, "sgn", [P, 2, DR])
            mask = sb(att, "mask", [P, S])
            rms_eps = sb(att, "rms_eps", [P, 1])
            mhalf = sb(att, "mhalf", [P, 2])
            x_raw = sb(att, "x_raw", [P, 2, S])
            x_hi = sb(att, "x_hi", [P, 2, S], F32R)
            x_lo = sb(att, "x_lo", [P, 2, S], F32R)
            x_nat = sb(att, "x_nat", [P, 2, D])
            sq = sb(att, "sq", [P, QL])
            ss = sb(att, "ss", [P, 2, 2])
            ms = sb(att, "ms", [P, 2, 2])
            rstd = sb(att, "rstd", [P, 2, 2])
            kr1 = sb(att, "kr1", [P, DR])
            kr2 = sb(att, "kr2", [P, DR])
            an = sb(att, "an", [P, 2, NA])
            cq_hi = [sb(att, f"cq_hi{i}", [P, 2, S], F32R) for i in range(2)]
            cq_lo = [sb(att, f"cq_lo{i}", [P, 2, S], F32R) for i in range(2)]
            kT = [sb(att, f"kT{i}", [P, S]) for i in range(2)]
            k_hi = [sb(att, f"k_hi{i}", [P, S], F32R) for i in range(2)]
            k_lo = [sb(att, f"k_lo{i}", [P, S], F32R) for i in range(2)]
            v0_hi = [sb(att, f"v0_hi{i}", [P, 3 * KL], F32R) for i in range(2)]
            v0_lo = [sb(att, f"v0_lo{i}", [P, 3 * KL], F32R) for i in range(2)]
            v1 = [sb(att, f"v1_{i}", [P, 3 * KL]) for i in range(2)]
            q_nat = [[sb(att, f"q_nat{i}{t}", [P, 4, P]) for t in range(2)] for i in range(2)]
            r1 = sb(att, "r1", [P, 4, DR])
            r2 = sb(att, "r2", [P, 4, DR])
            qT = [sb(att, f"qT{i}", [P, 2, P]) for i in range(2)]
            qT_hi = [sb(att, f"qT_hi{i}", [P, 2, P], F32R) for i in range(2)]
            qT_lo = [sb(att, f"qT_lo{i}", [P, 2, P], F32R) for i in range(2)]
            probs = [sb(att, f"probs{i}", [P, 2, 3 * P]) for i in range(2)]
            negmax = [sb(att, f"negmax{i}", [P, 4]) for i in range(2)]
            psums = [sb(att, f"psums{i}", [P, 4]) for i in range(2)]
            rden = [sb(att, f"rden{i}", [P, 4]) for i in range(2)]
            pT_hi = sb(att, "pT_hi", [P, 2, S], F32R)
            pT_lo = sb(att, "pT_lo", [P, 2, S], F32R)
            pT_k1 = sb(att, "pT_k1", [P, 2, P])
            ctx_hi = [sb(att, f"ctx_hi{i}", [P, S], F32R) for i in range(2)]
            ctx_lo = [sb(att, f"ctx_lo{i}", [P, S], F32R) for i in range(2)]
            xs = sb(att, "xs", [P, 2, D])
            bst = sb(att, "bst", [P, 2, 6])
            mv = sb(att, "mv", [P, 2, 2])
            vps = sb(att, "vps", [P, 2])
            lnr = sb(att, "lnr", [P, 2])

        ffn = top
        w_hi = [sb(ffn, f"w_hi{i}", [P, WCOLS], F32R) for i in range(2)]
        w_lo = [sb(ffn, f"w_lo{i}", [P, WCOLS], F32R) for i in range(2)]
        acc = sb(ffn, "acc", [P, TT, D])
        silu = sb(ffn, "silu", [P, 3, C])
        h32 = sb(ffn, "h32", [P, 3, C])
        h_hi = sb(ffn, "h_hi", [P, 3, C], F32R)
        h_lo = sb(ffn, "h_lo", [P, 3, C], F32R)
        wr_raw = sb(ffn, "wr_raw", [P, 2, P])
        wr_hi = sb(ffn, "wr_hi", [P, 2, P], F32R)
        wr_lo = sb(ffn, "wr_lo", [P, 2, P], F32R)
        lgT = sb(ffn, "lgT", [P, 2, C])
        logits = sb(ffn, "logits", [P, TT, E])
        rank = sb(ffn, "rank", [P, E])
        g_eq = sb(ffn, "g_eq", [P, TT, E])
        g_w = sb(ffn, "g_w", [P, TT, E])
        sel1 = sb(ffn, "sel1", [P, TT, E])
        sel2 = sb(ffn, "sel2", [P, TT, E])
        g_l2 = sb(ffn, "g_l2", [P, TT, E])
        g_m1 = sb(ffn, "g_m1", [P, TT])
        g_m2 = sb(ffn, "g_m2", [P, TT])
        g_r = sb(ffn, "g_r", [P, 2, TT])
        g_d = sb(ffn, "g_d", [P, TT])
        g_e = sb(ffn, "g_e", [P, TT])
        g_den = sb(ffn, "g_den", [P, TT])
        g_1 = sb(ffn, "g_1", [P, TT])
        g_2 = sb(ffn, "g_2", [P, TT])
        gates = sb(ffn, "gates", [P, TT, E])
        mhalf4 = sb(ffn, "mhalf4", [P, 4])
        bst2 = sb(ffn, "bst2", [P, 4, 6])
        mv2 = sb(ffn, "mv2", [P, 4, 2])
        vps2 = sb(ffn, "vps2", [P, 4])
        rs2 = sb(ffn, "rs2", [P, 4])
        mr2 = sb(ffn, "mr2", [P, 4])
        nb2 = sb(ffn, "nb2", [P, 4])

        b_q = bank("b_q")
        b_qT = bank("b_qT")
        b_s = [bank("b_s0"), bank("b_s1")]
        b_pT = bank("b_pT")
        b_c = bank("b_c")
        b_o = bank("b_o")
        b_x = bank("b_x")
        b_u, b_v, b_y = [b_q, b_qT, b_s[0]], [b_s[1], b_pT, b_c], [b_o, b_x]

        def live(u, lag, first, tail):
            return (not first or u >= lag) and (not tail or u < lag)

        def bodies(engine, step, tail_steps=BATCH_STEPS):
            for u in range(BODY):
                step(0, u, True, False, False)
            with engine.Fori(1, NB // 2 - 1) as B:
                for u in range(BODY):
                    step(B, u, False, False, False)
            for u in range(BODY):
                step(NB // 2 - 1, u, False, True, False)
            for u in range(tail_steps):
                step(NB // 2, u, False, False, True)

        def batch_of(B, u):
            return 2 * B + u // BATCH_STEPS, u % BATCH_STEPS

        def has_next(u, last, tail):
            return not tail and not (last and u >= BATCH_STEPS)

        def has_prev(u, first):
            return not (first and u < BATCH_STEPS)

        def above_zero(count):
            return not isinstance(count, int) or count > 0

        def hold_dve(column):
            nc.vector.memset(held[:, column:column + 1], 0.0)

        def hold_pool(column):
            nc.gpsimd.tensor_tensor(held[:, column:column + 1], held_in[:], held_in[:], ALU.add)

        block = top.enter_context(nc.Block())

        @block.sync
        def _(sp):
            sp.dma_start(wa_raw[:], waT.rearrange("(k p) n -> p k n", p=P)).then_inc(sem("wa_loaded"), 16)
            sp.dma_start(x_raw[:], xT[0].rearrange("(k p) n -> p k n", p=P)).then_inc(sem("xT_loaded"), 16)
            for i in range(2):
                sp.dma_start(cos[:, i], rope[0, i * P:(i + 1) * P]).then_inc(sem("rope_loaded"), 16)
                sp.dma_start(sgn[:, i], rope[1, i * P:(i + 1) * P]).then_inc(sem("rope_loaded"), 16)
            sp.dma_start(wq_nope[:], wqb.rearrange("(h c) r -> c h r", h=H)[0:DN]).then_inc(sem("wq_loaded"), 16)
            sp.dma_start(wq_pe[:, 0], wqbT.rearrange("r (h c) -> r h c", h=H)[0:P, :, DN:DQ]
                         ).then_inc(sem("wpe_loaded"), 16)
            sp.dma_start(wq_pe[0:QL - P, 1], wqbT.rearrange("r (h c) -> r h c", h=H)[P:QL, :, DN:DQ]
                         ).then_inc(sem("wpe_loaded"), 16)
            sp.dma_start(wo_t[:], woT.rearrange("(h p) n -> p h n", p=P)).then_inc(sem("wo_loaded"), 16)
            sp.dma_start(wraw[:], wffn[0]).then_inc(sem("wraw_loaded"), 16)

            def batch(b, head, rest):
                if rest:
                    sp.wait_ge(sem("xhi_done"), b + 1)
                    sp.wait_ge(sem("xlo_done"), b + 1)
                    sp.dma_start(x_raw[:], xT[b + 1].rearrange("(k p) n -> p k n", p=P)
                                 ).then_inc(sem("xT_loaded"), 16)
                if not head:
                    store_x1(b - 1)
                    sp.wait_ge(sem("ln_r"), b)
                sp.dma_start(x_nat[:], x[b].rearrange("(t p) n -> p t n", p=P)).then_inc(sem("xnat_loaded"), 16)

            def store_x1(b):
                sp.wait_ge(sem("ln_done"), 2 * (b + 1))
                sp.dma_start(x1_dram[b].rearrange("(t p) n -> p t n", p=P), xs[:]).then_inc(sem("x1_stored"), 16)

            batch(0, True, True)
            with sp.Fori(1, NB - 1) as b:
                batch(b, False, True)
            batch(NB - 1, False, False)
            store_x1(NB - 1)

            sp.wait_ge(sem("x1_stored"), 16 * NB)
            sp.wait_ge(sem("x1t_lo"), NB)
            x1_v = x1_dram.rearrange("b (t p) n -> p (b t) n", p=P)
            sp.dma_start(acc[:, 0:4], x1_v[:, 0:4]).then_inc(sem("acc0_loaded"), 16)
            sp.dma_start(acc[:, 4:TT], x1_v[:, 4:TT]).then_inc(sem("acc_loaded"), 16)

            def load_expert(e):
                sp.wait_ge(sem("w_hi_done"), PIECES * e)
                sp.wait_ge(sem("w_lo_done"), PIECES * e)
                sp.dma_start(wraw[:], wffn[e]).then_inc(sem("wraw_loaded"), 16)

            load_expert(1)
            with sp.Fori(2, E + 1) as e:
                load_expert(e)
            out_v = out.rearrange("b (t p) n -> p (b t) n", p=P)
            with sp.Fori(0, NC) as c:
                sp.wait_ge(sem("out_ready"), 4 * c + 4)
                sp.dma_start(out_v[:, bass.ds(4 * c, 4)], acc[:, bass.ds(4 * c, 4)]).then_inc(sem("out_stored"), 16)
            sp.wait_ge(sem("out_stored"), 16 * NC)

        @block.tensor
        def _(pe):
            def passes(out_ap, terms, start=True, stop=True, chk=False):
                for i, (w, m) in enumerate(terms):
                    mm = pe.matmul(out_ap, w, m, start=start and i == 0, stop=stop and i == len(terms) - 1,
                                   skip_group_check=chk)
                return mm

            def split3(w, m):
                return [(w[0], m[0]), (w[1], m[0]), (w[0], m[1])]

            def down(b, t):
                idx = 2 * b + t
                pe.wait_ge(sem("xhi_done"), b + 1)
                pe.wait_ge(sem("xlo_done"), b + 1)
                if t == 0:
                    if above_zero(b - 2):
                        pe.wait_ge(sem("x1t_hi"), b - 2)
                        pe.wait_ge(sem("x1t_lo"), b - 2)
                else:
                    pe.wait_ge(sem("cq_hi_done"), idx)
                    pe.wait_ge(sem("cq_lo_done"), idx)
                    pe.wait_ge(sem("kT_done"), idx)
                tt = slice(t * P, (t + 1) * P)
                terms = [z for k in range(2) for z in split3((x_hi[:, k, tt], x_lo[:, k, tt]),
                                                             (wa_hi[:, k], wa_lo[:, k]))]
                passes(b_x[:, 0:NA], terms).then_inc(sem("down_done"), 1)

            def down_T(b, t):
                idx = 2 * b + t
                pe.wait_ge(sem("an_done"), 2 * idx + 2)
                pe.wait_ge(sem("kpe_done"), idx + 1)
                pe.transpose(b_x[:, 0:P], an[:, t, 0:P], ident[:])
                pe.transpose(b_x[:, P:2 * P], an[:, t, P:2 * P], ident[:])
                pe.transpose(b_x[:, 2 * P:3 * P], an[:, t, NA - P:NA], ident[:]).then_inc(sem("downT_done"), 1)

            def x1_T(b):
                pe.wait_ge(sem("ln_done"), 2 * (b + 1))
                for k in range(2):
                    for t in range(2):
                        mm = pe.transpose(b_x[:, (2 * k + t) * P:(2 * k + t + 1) * P],
                                          xs[:, t, k * P:(k + 1) * P], ident[:])
                mm.then_inc(sem("x1T_done"), 1)

            pe.wait_ge(sem("wa_hi_done"), 1)
            pe.wait_ge(sem("wa_lo_done"), 1)
            down(0, 0)
            pe.wait_ge(sem("wq_loaded"), 16)
            pe.wait_ge(sem("wkv_loaded"), 32)
            for k, rows in ((0, P), (1, QL - P)):
                for g in range(2):
                    dst = (b_q, b_qT, b_s[0], b_s[1])[2 * k + g]
                    for i in range(8):
                        h = 8 * g + i
                        mm = pe.matmul(dst[0:rows, i * KL:(i + 1) * KL], wq_nope[:, h, k * P:k * P + rows],
                                       wk_nat[:, h], start=True, stop=True)
                    mm.then_inc(sem("wm_done"), 1)
            pe.wait_ge(sem("ident_done"), 1)
            down_T(0, 0)
            down(0, 1)
            pe.wait_ge(sem("wo_loaded"), 16)

            def value_out(g, dst):
                for i in range(2):
                    for hh in range(2):
                        h = 4 * g + 2 * i + hh
                        mm = pe.matmul(dst[hh * KL:(hh + 1) * KL, i * D:(i + 1) * D], wv_nat[:, h], wo_t[:, h],
                                       start=True, stop=True)
                mm.then_inc(sem("wvo_done"), 1)

            for g, dst in enumerate((b_pT, b_c, b_o)):
                value_out(g, dst)
            down_T(0, 1)
            pe.wait_ge(sem("cq_hi_done"), 2)
            pe.wait_ge(sem("cq_lo_done"), 2)
            pe.wait_ge(sem("kT_done"), 2)
            value_out(3, b_x)
            pe.wait_ge(sem("prep_hi"), 10)
            pe.wait_ge(sem("prep_lo"), 10)

            def step(B, u, first, last, tail):
                s = BODY * B + u
                b, p = batch_of(B, u)
                if live(u, LAG_PV, first, tail):
                    q = s - LAG_PV
                    pe.wait_ge(sem("norm_done"), 4 * q + 4)
                    if above_zero(q):
                        pe.wait_ge(sem("pT_hi_done"), q)
                        pe.wait_ge(sem("pT_lo_done"), q)
                        pe.wait_ge(sem("ctx_hi_done"), q)
                        pe.wait_ge(sem("ctx_lo_done"), q)
                    pr = probs[(u - LAG_PV) % 2]
                    for h in range(2):
                        for t in range(2):
                            pe.transpose(b_pT[:, h * S + t * P:h * S + (t + 1) * P], pr[:, h, t * P:(t + 1) * P],
                                         ident[:])
                    for h in range(2):
                        mm = pe.transpose(b_c[:, h * P:(h + 1) * P], pr[:, h, 2 * P:3 * P], ident[:])
                    mm.then_inc(sem("pT_done"), 1)
                if not tail:
                    t, quad, par = u % 2, (u // 2) % 4, (u // BATCH_STEPS) % 2
                    if above_zero(s):
                        pe.wait_ge(sem("qlat_done"), s)
                        pe.wait_ge(sem("rope_done"), s)
                    if p == 0:
                        pe.wait_ge(sem("cq_hi_done"), 2 * b + 2)
                        pe.wait_ge(sem("cq_lo_done"), 2 * b + 2)
                    tt = slice(t * P, (t + 1) * P)
                    terms = []
                    for k, rows in ((0, P), (1, QL - P)):
                        hs = slice(4 * quad, 4 * quad + 4)
                        terms += split3((cq_hi[par][0:rows, k, tt], cq_lo[par][0:rows, k, tt]),
                                        (m_hi[0:rows, k, hs], m_lo[0:rows, k, hs]))
                    passes(b_q[:], terms).then_inc(sem("q_done"), 1)
                if live(u, LAG_PV, first, tail):
                    q, par = s - LAG_PV, ((u - LAG_PV) // BATCH_STEPS) % 2
                    pe.wait_ge(sem("pT_hi_done"), q + 1)
                    pe.wait_ge(sem("pT_k1_done"), q + 1)
                    if (u - LAG_PV) % BATCH_STEPS == 0:
                        bq = (2 * B + (u - LAG_PV) // BATCH_STEPS)
                        pe.wait_ge(sem("v0_hi_done"), bq + 1)
                        pe.wait_ge(sem("v0_lo_done"), bq + 1)
                        pe.wait_ge(sem("v1_done"), bq + 1)
                    cols = [slice(KL, 3 * KL), slice(0, 2 * KL)]
                    c_ap = b_c[:, S:2 * S]
                    for h in range(2):
                        passes(c_ap, [(v0_hi[par][:, cols[h]], pT_hi[:, h]), (v0_lo[par][:, cols[h]], pT_hi[:, h])],
                               start=(h == 0), stop=False, chk=True)
                    for h in range(2):
                        passes(b_c[:, S + P:2 * S], [(v1[par][:, cols[h]], pT_k1[:, h])], start=False, stop=False,
                               chk=True)
                    pe.wait_ge(sem("pT_lo_done"), q + 1)
                    for h in range(2):
                        mm = passes(c_ap, [(v0_hi[par][:, cols[h]], pT_lo[:, h])], start=False, stop=(h == 1),
                                    chk=True)
                    mm.then_inc(sem("ctx_done"), 1)
                if live(u, LAG_WO, first, tail):
                    q, pq = s - LAG_WO, (u - LAG_WO) % BATCH_STEPS
                    pe.wait_ge(sem("ctx_hi_done"), q + 1)
                    pe.wait_ge(sem("ctx_lo_done"), q + 1)
                    if pq == 0:
                        if above_zero(2 * B + (u - LAG_WO) // BATCH_STEPS):
                            pe.wait_ge(sem("ln_r"), 2 * B + (u - LAG_WO) // BATCH_STEPS)
                    cp = (u - LAG_WO) % 2
                    for t in range(2):
                        tt = slice(t * P, (t + 1) * P)
                        mm = passes(b_o[:, t * D:(t + 1) * D],
                                    split3((ctx_hi[cp][:, tt], ctx_lo[cp][:, tt]),
                                           (wvo_hi[:, pq], wvo_lo[:, pq])),
                                    start=(pq == 0 and t == 0), stop=(pq == PAIRS - 1), chk=True)
                    mm.then_inc(sem("o_done"), 1)
                if p in (2, 4) and has_next(u, last, tail):
                    down(b + 1, p // 2 - 1)
                if p in (3, 5) and has_next(u, last, tail):
                    down_T(b + 1, p // 2 - 1)
                if p == 7 and has_prev(u, first):
                    n_down = 2 * (b + 2) if has_next(u, last, tail) else 2 * NB
                    pe.wait_ge(sem("cq_hi_done"), n_down)
                    pe.wait_ge(sem("cq_lo_done"), n_down)
                    pe.wait_ge(sem("kT_done"), n_down)
                    x1_T(b - 1)
                if live(u, LAG_QT, first, tail):
                    q, j = s - LAG_QT, (u % 2) * 2
                    qn = q_nat[((u - LAG_QT) // 2) % 2]
                    need = s if u % 2 == 0 else s - 1
                    pe.wait_ge(sem("qlat_done"), need)
                    pe.wait_ge(sem("qrope_done"), need)
                    if above_zero(q):
                        pe.wait_ge(sem("qT_done"), q)
                        pe.wait_ge(sem("qT_hi_done"), q)
                        pe.wait_ge(sem("qT_lo_done"), q)
                    for t in range(2):
                        for h in range(2):
                            mm = pe.transpose(b_qT[:, (2 * t + h) * P:(2 * t + h + 1) * P], qn[t][:, j + h], ident[:])
                    mm.then_inc(sem("qTb_done"), 1)
                if live(u, LAG_SC, first, tail):
                    q, i, par = s - LAG_SC, (u - LAG_SC) % 2, ((u - LAG_SC) // BATCH_STEPS) % 2
                    pe.wait_ge(sem("qT_done"), q + 1)
                    pe.wait_ge(sem("qT_hi_done"), q + 1)
                    pe.wait_ge(sem("qT_lo_done"), q + 1)
                    if (u - LAG_SC) % BATCH_STEPS == 0:
                        bq = 2 * B + (u - LAG_SC) // BATCH_STEPS
                        pe.wait_ge(sem("kT_done"), 2 * bq + 2)
                        pe.wait_ge(sem("k_hi_done"), 2 * bq + 2)
                        pe.wait_ge(sem("k_lo_done"), 2 * bq + 2)
                    if above_zero(4 * q):
                        pe.wait_ge(sem("masked_done"), 4 * q)
                    for h in range(2):
                        pe.matmul(b_s[h][:, 0:P], qT[i][:, h], kT[par][:, 0:P], start=True, stop=True)
                        mm = passes(b_s[h][:, P:3 * P], split3((qT_hi[i][:, h], qT_lo[i][:, h]),
                                                               (k_hi[par][:], k_lo[par][:])))
                    mm.then_inc(sem("s_done"), 1)

            bodies(pe, step)

            pe.wait_ge(sem("wr_hi_done"), 1)
            pe.wait_ge(sem("wr_lo_done"), 1)
            pe.wait_ge(sem("x1t_hi"), NB)
            pe.wait_ge(sem("x1t_lo"), NB)

            def router_T(c):
                if above_zero(c - 1):
                    pe.wait_ge(sem("lg_read"), c - 1)
                pe.wait_ge(sem("lgT_done"), c + 1)
                for t in range(4):
                    mm = pe.transpose(b_v[c % 2][:, t * P:(t + 1) * P], lgT[:, c % 2, t * P:(t + 1) * P], ident[:])
                mm.then_inc(sem("lg_done"), 1)

            for c in range(NC):
                if above_zero(c - 1):
                    pe.wait_ge(sem("lgT_done"), c - 1)
                cc = slice(c * C, (c + 1) * C)
                terms = [z for k in range(2) for z in split3((wr_hi[:, k], wr_lo[:, k]),
                                                             (x1T_hi[:, k, cc], x1T_lo[:, k, cc]))]
                passes(b_u[c % 2][:], terms).then_inc(sem("lgTb_done"), 1)
                if c >= 1:
                    router_T(c - 1)
            router_T(NC - 1)
            pe.wait_ge(sem("lg_read"), NC)

            def up(n, c, par, m, before):
                if before:
                    pe.wait_ge(sem("silu_done"), 3 * (n - 1) + m + 1)
                    pe.wait_ge(sem("h32_done"), 3 * (n - 1) + m + 1)
                w = MT[m]
                for bk, base in ((b_u[m], 0), (b_v[m], W3_AT)):
                    terms = []
                    for k in range(2):
                        a = base + k * HF + m * P
                        xc = (x1T_hi[:, k, bass.ds(c * C, C)], x1T_lo[:, k, bass.ds(c * C, C)])
                        terms += split3((w_hi[par][:, a:a + w], w_lo[par][:, a:a + w]), xc)
                    mm = passes(bk[0:w, :], terms)
                mm.then_inc(sem("up_done"), 1)

            def y_out(n, par, before):
                for j in range(2):
                    if before:
                        pe.wait_ge(sem("y_added"), 2 * (n - 1) + j + 1)
                    for k in range(3):
                        pe.wait_ge(sem("h_hi_done"), 3 * n + k + 1)
                        pe.wait_ge(sem("h_lo_done"), 3 * n + k + 1)
                        w = MT[k]
                        for t in range(2):
                            tt = slice((2 * j + t) * P, (2 * j + t + 1) * P)
                            a = W2_AT + k * D
                            mm = passes(b_y[j][:, t * D:(t + 1) * D],
                                        split3((h_hi[0:w, k, tt], h_lo[0:w, k, tt]),
                                               (w_hi[par][0:w, a:a + D], w_lo[par][0:w, a:a + D])),
                                        start=(k == 0 and t == 0), stop=(k == 2), chk=True)
                    mm.then_inc(sem("y_done"), 1)

            def chunk(e, c, par, before, before2):
                n = NC * e + c
                up(n, c, par, 0, before)
                if before:
                    first_chunk = isinstance(c, int) and c == 0
                    y_out(n - 1, 1 - par if first_chunk else par, before2)
                up(n, c, par, 1, before)
                up(n, c, par, 2, before)

            def expert(e, par):
                pe.wait_ge(sem("w_hi_done"), PIECES * (e + 1))
                pe.wait_ge(sem("w_lo_done"), PIECES * (e + 1))
                chunk(e, 0, par, True, True)
                with pe.Fori(1, NC) as c:
                    chunk(e, c, par, True, True)

            pe.wait_ge(sem("w_hi_done"), PIECES)
            pe.wait_ge(sem("w_lo_done"), PIECES)
            chunk(0, 0, 0, False, False)
            chunk(0, 1, 0, True, False)
            with pe.Fori(2, NC) as c:
                chunk(0, c, 0, True, True)
            with pe.Fori(0, E // 2 - 1) as j:
                expert(2 * j + 1, 1)
                expert(2 * j + 2, 0)
            expert(E - 1, 1)
            expert(E, 0)
            y_out(NC * (E + 1) - 1, 0, True)

        @block.scalar
        def _(act):
            act.dma_start(wk_nat[:], wkvb.rearrange("(h c) r -> c h r", h=H)[0:DN]).then_inc(sem("wkv_loaded"), 16)
            act.dma_start(wv_nat[:], wkvb.rearrange("(h c) r -> c h r", h=H)[DN:DN + DV]
                          ).then_inc(sem("wkv_loaded"), 16)
            with nc.allow_non_contiguous_dma(reason="norm weights, one value to a partition"):
                act.dma_start(aln_c[:, 0:1], aln[0:P].unsqueeze(1)).then_inc(sem("ln_w_loaded"), 16)
                act.dma_start(aln_c[0:QL - P, 1:2], aln[P:QL].unsqueeze(1)).then_inc(sem("ln_w_loaded"), 16)
                act.dma_start(kvln2[0:KL], kvln.unsqueeze(1)).then_inc(sem("ln_w_loaded"), 16)
                act.dma_start(kvln2[KL:P], kvln.unsqueeze(1)).then_inc(sem("ln_w_loaded"), 16)
                act.dma_start(kvln1[0:KL], kvln.unsqueeze(1)).then_inc(sem("ln_w_loaded"), 16)

            def squares(b, t):
                idx = 2 * b + t
                act.wait_ge(sem("down_done"), idx + 1)
                if above_zero(idx - 1):
                    act.wait_ge(sem("rstd_done"), idx - 1)
                act.activation(sq[:, 0:QL], b_x[:, 0:QL], ACT.Square, scale=float(QL) ** -0.5,
                               accum_out=ss[:, t, 0:1]).then_inc(sem("ss_done"), 1)
                act.wait_ge(sem("ss_done"), 2 * idx + 1)
                act.activation(sq[:, 0:KL], b_x[:, QL:QL + KL], ACT.Square, scale=float(KL) ** -0.5,
                               accum_out=ss[:, t, 1:2]).then_inc(sem("ss_done"), 1)

            def normed(b, t):
                idx = 2 * b + t
                act.wait_ge(sem("rstd_done"), idx + 1)
                act.wait_ge(sem("kpe_done"), idx + 1)
                if above_zero(idx - 1):
                    act.wait_ge(sem("downT_done"), idx - 1)
                if above_zero(b):
                    act.wait_ge(sem("v0_hi_done"), b)
                    act.wait_ge(sem("v0_lo_done"), b)
                    act.wait_ge(sem("v1_done"), b)
                act.activation(an[:, t, 0:QL], b_x[:, 0:QL], ACT.Copy, scale=rstd[:, t, 0:1]
                               ).then_inc(sem("an_done"), 1)
                act.activation(an[:, t, QL:QL + KL], b_x[:, QL:QL + KL], ACT.Copy, scale=rstd[:, t, 1:2]
                               ).then_inc(sem("an_done"), 1)

            def down_hi(b, t, par):
                idx = 2 * b + t
                act.wait_ge(sem("downT_done"), idx + 1)
                if above_zero(BATCH_STEPS * (b - 1)):
                    act.wait_ge(sem("q_done"), BATCH_STEPS * (b - 1))
                    act.wait_ge(sem("s_done"), BATCH_STEPS * (b - 1))
                tt = slice(t * P, (t + 1) * P)
                act.activation(cq_hi[par][:, :, tt], b_x[:, 0:2 * P].rearrange("p (k n) -> p k n", k=2), ACT.Copy
                               ).then_inc(sem("cq_hi_done"), 1)
                act.activation(kT[par][:, tt], b_x[:, 2 * P:3 * P], ACT.Copy, scale=kvln1[:]
                               ).then_inc(sem("kT_done"), 1)

            act.wait_ge(sem("ln_w_loaded"), 80)
            act.wait_ge(sem("ones_done"), 1)
            for t in range(2):
                squares(0, t)
                normed(0, t)
                down_hi(0, t, 0)
            for k, rows in ((0, P), (1, QL - P)):
                for g in range(2):
                    i = 2 * k + g
                    src = (b_q, b_qT, b_s[0], b_s[1])[i]
                    act.wait_ge(sem("wm_done"), i + 1)
                    act.activation(m_hi[0:rows, k, 8 * g:8 * g + 8, 0:KL],
                                   src[0:rows, :].rearrange("p (h c) -> p h c", h=8), ACT.Copy,
                                   scale=aln_c[0:rows, k:k + 1]).then_inc(sem("prep_hi"), 1)
            act.wait_ge(sem("wpe_loaded"), 32)
            for k, rows in ((0, P), (1, QL - P)):
                act.activation(m_hi[0:rows, k, :, KL:P], wq_pe[0:rows, k], ACT.Copy, scale=aln_c[0:rows, k:k + 1]
                               ).then_inc(sem("prep_hi"), 1)
            for g, src in enumerate((b_pT, b_c, b_o, b_x)):
                act.wait_ge(sem("wvo_done"), g + 1)
                act.activation(wvo_hi[:, 2 * g:2 * g + 2], src[:].rearrange("p (i n) -> p i n", i=2), ACT.Copy,
                               scale=kvln2[:]).then_inc(sem("prep_hi"), 1)

            def step(B, u, first, last, tail):
                s = BODY * B + u
                b, p = batch_of(B, u)
                if p in (3, 5) and has_next(u, last, tail):
                    normed(b + 1, p // 2 - 1)
                if live(u, LAG_PV, first, tail):
                    q = s - LAG_PV
                    act.wait_ge(sem("pT_done"), q + 1)
                    if above_zero(q):
                        act.wait_ge(sem("ctx_done"), q)
                    act.activation(pT_hi[:], b_pT[:].rearrange("p (h n) -> p h n", h=2), ACT.Copy
                                   ).then_inc(sem("pT_hi_done"), 1)
                    act.activation(pT_k1[:], b_c[:, 0:2 * P].rearrange("p (h n) -> p h n", h=2), ACT.Copy
                                   ).then_inc(sem("pT_k1_done"), 1)
                if live(u, LAG_SM, first, tail):
                    q, i = s - LAG_SM, (u - LAG_SM) % 2
                    if above_zero(q - 1):
                        act.wait_ge(sem("rden_done"), q - 1)
                    for h in range(2):
                        for t in range(2):
                            z = 2 * h + t
                            act.wait_ge(sem("masked_done"), 4 * q + z + 1)
                            sc = probs[i][:, h, 0:P] if t == 0 else probs[i][:, h, P:3 * P]
                            act.activation(sc, sc, ACT.Exp, bias=negmax[i][:, z:z + 1], scale=-1.0,
                                           accum_out=psums[i][:, z:z + 1]).then_inc(sem("exp_done"), 1)
                if not tail:
                    t, qp = u % 2, (u // 2) % 2
                    act.wait_ge(sem("q_done"), s + 1)
                    if not (first and u < 4):
                        act.wait_ge(sem("qTb_done"), s - t - 2)
                    act.activation(q_nat[qp][t][:, :, 0:KL], b_q[:].rearrange("p (h c) -> p h c", h=4)[:, :, 0:KL],
                                   ACT.Copy).then_inc(sem("qlat_done"), 1)
                if live(u, LAG_PV, first, tail):
                    q, cp = s - LAG_PV, (u - LAG_PV) % 2
                    act.wait_ge(sem("ctx_done"), q + 1)
                    if above_zero(q - 1):
                        act.wait_ge(sem("o_done"), q - 1)
                    act.activation(ctx_hi[cp][:], b_c[:, S:2 * S], ACT.Copy).then_inc(sem("ctx_hi_done"), 1)
                if p in (2, 4) and has_next(u, last, tail):
                    squares(b + 1, p // 2 - 1)
                if p in (3, 5) and has_next(u, last, tail):
                    down_hi(b + 1, p // 2 - 1, (u // BATCH_STEPS + 1) % 2)
                if p == 7 and has_prev(u, first):
                    act.wait_ge(sem("x1T_done"), b)
                    act.activation(x1T_hi[:, :, bass.ds((b - 1) * S, S)], b_x[:].rearrange("p (k n) -> p k n", k=2),
                                   ACT.Copy).then_inc(sem("x1t_hi"), 1)
                if live(u, LAG_QT, first, tail):
                    q, i = s - LAG_QT, (u - LAG_QT) % 2
                    act.wait_ge(sem("qTb_done"), q + 1)
                    if above_zero(q - 1):
                        act.wait_ge(sem("s_done"), q - 1)
                    act.activation(qT[i][:], b_qT[:, 0:S].rearrange("p (h n) -> p h n", h=2), ACT.Copy
                                   ).then_inc(sem("qT_done"), 1)
                    act.activation(qT_hi[i][:], b_qT[:, S:2 * S].rearrange("p (h n) -> p h n", h=2), ACT.Copy
                                   ).then_inc(sem("qT_hi_done"), 1)

            bodies(act, step)

            for c in range(NC):
                act.wait_ge(sem("lgTb_done"), c + 1)
                if c == 0:
                    act.wait_ge(sem("x1t_lo"), NB)
                    act.wait_ge(sem("x1_stored"), 16 * NB)
                if above_zero(c - 1):
                    act.wait_ge(sem("lg_done"), c - 1)
                act.activation(lgT[:, c % 2], b_u[c % 2][:], ACT.Copy).then_inc(sem("lgT_done"), 1)

            def chunk(n, before):
                for m in range(3):
                    w = MT[m]
                    act.wait_ge(sem("up_done"), 3 * n + m + 1)
                    if before:
                        act.wait_ge(sem("h32_done"), 3 * (n - 1) + m + 1)
                    act.activation(silu[0:w, m], b_u[m][0:w, :], ACT.Silu).then_inc(sem("silu_done"), 1)
                    act.wait_ge(sem("h32_done"), 3 * n + m + 1)
                    if before:
                        act.wait_ge(sem("y_done"), 2 * n)
                    act.activation(h_hi[0:w, m], h32[0:w, m], ACT.Copy).then_inc(sem("h_hi_done"), 1)

            def finish(c):
                for t in range(4):
                    act.wait_ge(sem("ln2_done"), c + 1)
                    a = acc[:, bass.ds(4 * c + t, 1)].rearrange("p a n -> p (a n)")
                    act.activation(a, a, ACT.Identity, bias=nb2[:, t:t + 1], scale=rs2[:, t:t + 1]
                                   ).then_inc(sem("out_ready"), 1)

            def split_piece(e, c, par):
                act.wait_ge(sem("wraw_loaded"), 16 * (e + 2))
                if above_zero(2 * NC * e):
                    act.wait_ge(sem("y_done"), 2 * NC * e)
                pc = bass.ds((c - 1) * PIECE, PIECE)
                act.activation(w_hi[par][:, pc], wraw[:, pc], ACT.Copy).then_inc(sem("w_hi_done"), 1)

            def expert(e, par):
                chunk(NC * e, True)
                with act.Fori(1, NC) as c:
                    chunk(NC * e + c, True)
                    split_piece(e, c, 1 - par)

            chunk(0, False)
            act.wait_ge(sem("g_diff"), 1)
            act.activation(g_e[:], g_d[:], ACT.Exp).then_inc(sem("g_exp"), 1)
            with act.Fori(1, NC) as c:
                chunk(c, True)
                split_piece(0, c, 1)
            expert(1, 1)
            with act.Fori(1, E // 2) as j:
                expert(2 * j, 0)
                expert(2 * j + 1, 1)
            chunk(NC * E, True)
            with act.Fori(1, NC) as c:
                chunk(NC * E + c, True)
                finish(c - 1)
            finish(NC - 1)

        @block.vector
        def _(dve):
            def lo(out_ap, full, hi, name):
                dve.tensor_tensor(out_ap, full, hi.bitcast(F32), ALU.subtract).then_inc(sem(name), 1)

            def x_low(b):
                dve.wait_ge(sem("xT_loaded"), 16 * (b + 1))
                dve.wait_ge(sem("xhi_done"), b + 1)
                if above_zero(2 * b):
                    dve.wait_ge(sem("down_done"), 2 * b)
                lo(x_lo[:], x_raw[:], x_hi[:], "xlo_done")

            def key_rope(b, t):
                idx = 2 * b + t
                dve.wait_ge(sem("ss_done"), 2 * idx + 2)
                if above_zero(idx - 1):
                    dve.wait_ge(sem("downT_done"), idx - 1)
                if above_zero(idx):
                    dve.wait_ge(sem("kpe_done"), idx)
                a = QL + KL
                hd = DR // 2
                dve.tensor_tensor(kr1[:], b_x[:, a:NA], cos[:, t], ALU.mult)
                dve.tensor_tensor(kr2[:, 0:hd], b_x[:, a + hd:NA], sgn[:, t, 0:hd], ALU.mult)
                dve.tensor_tensor(kr2[:, hd:DR], b_x[:, a:a + hd], sgn[:, t, hd:DR], ALU.mult
                                  ).then_inc(sem("kr_done"), 1)
                dve.wait_ge(sem("kr_done"), idx + 1)
                dve.tensor_tensor(an[:, t, a:NA], kr1[:], kr2[:], ALU.add).then_inc(sem("kpe_done"), 1)

            def cq_low(b, t, par):
                idx = 2 * b + t
                dve.wait_ge(sem("cq_hi_done"), idx + 1)
                dve.wait_ge(sem("kT_done"), idx + 1)
                if above_zero(BATCH_STEPS * (b - 1)):
                    dve.wait_ge(sem("q_done"), BATCH_STEPS * (b - 1))
                tt = slice(t * P, (t + 1) * P)
                lo(cq_lo[par][:, :, tt], b_x[:, 0:2 * P].rearrange("p (k n) -> p k n", k=2), cq_hi[par][:, :, tt],
                   "cq_lo_done")

            def k_low(b, t, par):
                tt = slice(t * P, (t + 1) * P)
                dve.wait_ge(sem("k_hi_done"), 2 * b + t + 1)
                if above_zero(BATCH_STEPS * (b - 1)):
                    dve.wait_ge(sem("s_done"), BATCH_STEPS * (b - 1))
                lo(k_lo[par][:, tt], kT[par][:, tt], k_hi[par][:, tt], "k_lo_done")

            def v_low(b, par):
                dve.wait_ge(sem("v0_hi_done"), b + 1)
                if above_zero(BATCH_STEPS * (b - 1)):
                    dve.wait_ge(sem("ctx_done"), BATCH_STEPS * (b - 1))
                dve.wait_ge(sem("pads_done"), 1)
                lo(v0_lo[par][:, KL:2 * KL], an[:, 0, QL:QL + KL], v0_hi[par][:, KL:2 * KL], "v0_lo_done")

            dve.memset(kvln1[KL:P], 1.0).then_inc(sem("ones_done"), 1)
            dve.wait_ge(sem("wa_loaded"), 16)
            dve.wait_ge(sem("wa_hi_done"), 1)
            lo(wa_lo[:], wa_raw[:], wa_hi[:], "wa_lo_done")
            x_low(0)
            dve.wait_ge(sem("rope_loaded"), 64)
            for t in range(2):
                key_rope(0, t)
                cq_low(0, t, 0)
                k_low(0, t, 0)
            v_low(0, 0)
            dve.wait_ge(sem("ln_w_loaded"), 80)

            def prep_low(i, dst, src, scale, hi):
                dve.wait_ge(sem("prep_hi"), i)
                dve.scalar_tensor_tensor(out=dst, in0=src, scalar=scale, in1=hi.bitcast(F32), op0=ALU.mult,
                                         op1=ALU.subtract).then_inc(sem("prep_lo"), 1)

            for k, rows in ((0, P), (1, QL - P)):
                for g in range(2):
                    i = 2 * k + g
                    prep_low(i + 1, m_lo[0:rows, k, 8 * g:8 * g + 8, 0:KL],
                             (b_q, b_qT, b_s[0], b_s[1])[i][0:rows, :].rearrange("p (h c) -> p h c", h=8),
                             aln_c[0:rows, k:k + 1], m_hi[0:rows, k, 8 * g:8 * g + 8, 0:KL])
            dve.wait_ge(sem("wpe_loaded"), 32)
            for k, rows in ((0, P), (1, QL - P)):
                prep_low(5 + k, m_lo[0:rows, k, :, KL:P], wq_pe[0:rows, k], aln_c[0:rows, k:k + 1],
                         m_hi[0:rows, k, :, KL:P])
            for g, src in enumerate((b_pT, b_c, b_o, b_x)):
                prep_low(7 + g, wvo_lo[:, 2 * g:2 * g + 2], src[:].rearrange("p (i n) -> p i n", i=2), kvln2[:],
                         wvo_hi[:, 2 * g:2 * g + 2])
            dve.wait_ge(sem("mask_done"), 1)

            def step(B, u, first, last, tail):
                s = BODY * B + u
                b, p = batch_of(B, u)
                npar = (u // BATCH_STEPS + 1) % 2
                if has_next(u, last, tail):
                    if p == 0:
                        x_low(b + 1)
                    if p in (4, 6):
                        k_low(b + 1, p // 2 - 2, npar)
                    if p == 7:
                        v_low(b + 1, npar)
                if p == 6 and has_prev(u, first):
                    dve.wait_ge(sem("lnr_done"), b)
                    for t in range(2):
                        dve.tensor_scalar(xs[:, t], xs[:, t], mv[:, t, 0:1], lnr[:, t:t + 1], ALU.subtract, ALU.mult
                                          ).then_inc(sem("ln_done"), 1)
                if live(u, LAG_PV, first, tail):
                    q = s - LAG_PV
                    dve.wait_ge(sem("pT_hi_done"), q + 1)
                    if above_zero(q):
                        dve.wait_ge(sem("ctx_done"), q)
                    lo(pT_lo[:], b_pT[:].rearrange("p (h n) -> p h n", h=2), pT_hi[:], "pT_lo_done")
                if live(u, LAG_SM, first, tail):
                    q, i = s - LAG_SM, (u - LAG_SM) % 2
                    dve.wait_ge(sem("exp_done"), 4 * q + 4)
                    if above_zero(4 * (q - 1)):
                        dve.wait_ge(sem("norm_done"), 4 * (q - 1))
                    dve.reciprocal(rden[i][:], psums[i][:]).then_inc(sem("rden_done"), 1)
                if not tail:
                    t = u % 2
                    dve.wait_ge(sem("qlat_done"), s + 1)
                    if above_zero(s):
                        dve.wait_ge(sem("qrope_done"), s)
                    hd = DR // 2
                    bq = b_q[:].rearrange("p (h c) -> p h c", h=4)
                    dve.tensor_tensor(r1[:], bq[:, :, KL:P], cos[:, t].unsqueeze(1).to_broadcast([P, 4, DR]), ALU.mult)
                    dve.tensor_tensor(r2[:, :, 0:hd], bq[:, :, KL + hd:P],
                                      sgn[:, t, 0:hd].unsqueeze(1).to_broadcast([P, 4, hd]), ALU.mult)
                    dve.tensor_tensor(r2[:, :, hd:DR], bq[:, :, KL:KL + hd],
                                      sgn[:, t, hd:DR].unsqueeze(1).to_broadcast([P, 4, hd]), ALU.mult
                                      ).then_inc(sem("rope_done"), 1)
                if live(u, LAG_PV, first, tail):
                    q, cp = s - LAG_PV, (u - LAG_PV) % 2
                    dve.wait_ge(sem("ctx_hi_done"), q + 1)
                    if above_zero(q - 1):
                        dve.wait_ge(sem("o_done"), q - 1)
                    lo(ctx_lo[cp][:], b_c[:, S:2 * S], ctx_hi[cp][:], "ctx_lo_done")
                if p in (2, 4) and has_next(u, last, tail):
                    key_rope(b + 1, p // 2 - 1)
                if p in (3, 5) and has_next(u, last, tail):
                    cq_low(b + 1, p // 2 - 1, npar)
                if p == 5 and has_prev(u, first):
                    dve.wait_ge(sem("o_done"), BATCH_STEPS * b)
                    dve.wait_ge(sem("xnat_loaded"), 16 * b)
                    if above_zero(b - 1):
                        dve.wait_ge(sem("x1T_done"), b - 1)
                    if above_zero(16 * (b - 1)):
                        dve.wait_ge(sem("x1_stored"), 16 * (b - 1))
                    if above_zero(2 * (b - 1)):
                        dve.wait_ge(sem("ln_done"), 2 * (b - 1))
                    dve.tensor_tensor(xs[:], b_o[:].rearrange("p (t n) -> p t n", t=2), x_nat[:], ALU.add
                                      ).then_inc(sem("ln_r"), 1)
                    dve.wait_ge(sem("ln_r"), b)
                    if above_zero(2 * (b - 1)):
                        dve.wait_ge(sem("bst_done"), 2 * (b - 1))
                    hold_dve(8)
                    for t in range(2):
                        dve.bn_stats(bst[:, t], xs[:, t]).then_inc(sem("bst_done"), 1)
                    for t in range(2):
                        dve.wait_ge(sem("bst_done"), 2 * b - 1 + t)
                        if above_zero(2 * (b - 1) + t):
                            dve.wait_ge(sem("mv_done"), 2 * (b - 1) + t)
                        hold_dve(9)
                        dve.bn_aggr(mv[:, t], bst[:, t]).then_inc(sem("mv_done"), 1)
                if p == 7 and has_prev(u, first):
                    dve.wait_ge(sem("x1t_hi"), b)
                    lo(x1T_lo[:, :, bass.ds((b - 1) * S, S)], b_x[:].rearrange("p (k n) -> p k n", k=2),
                       x1T_hi[:, :, bass.ds((b - 1) * S, S)], "x1t_lo")
                if live(u, LAG_QT, first, tail):
                    q, i = s - LAG_QT, (u - LAG_QT) % 2
                    dve.wait_ge(sem("qT_hi_done"), q + 1)
                    if above_zero(q - 1):
                        dve.wait_ge(sem("s_done"), q - 1)
                    lo(qT_lo[i][:], b_qT[:, S:2 * S].rearrange("p (h n) -> p h n", h=2), qT_hi[i][:], "qT_lo_done")
                if live(u, LAG_SC, first, tail):
                    q, i = s - LAG_SC, (u - LAG_SC) % 2
                    dve.wait_ge(sem("s_done"), q + 1)
                    if above_zero(q - 1):
                        dve.wait_ge(sem("pT_done"), q - 1)
                    if above_zero(4 * (q - 1)):
                        dve.wait_ge(sem("exp_done"), 4 * (q - 1))
                    if above_zero(4 * q):
                        dve.wait_ge(sem("masked_done"), 4 * q)
                    hold_dve(10)
                    for h in range(2):
                        for t in range(2):
                            cols = slice(0, P) if t == 0 else slice(P, 3 * P)
                            mk = mask[:, P:S] if t == 0 else mask[:]
                            dve.tensor_tensor_reduce(out=probs[i][:, h, cols], in0=b_s[h][:, cols], in1=mk,
                                                     scale=-SCALE, scalar=3e38, op0=ALU.add, op1=ALU.min,
                                                     accum_out=negmax[i][:, 2 * h + t:2 * h + t + 1]
                                                     ).then_inc(sem("masked_done"), 1)

            bodies(dve, step)

            dve.wait_ge(sem("w_hi_done"), 1)
            for i in range(PIECES):
                dve.wait_ge(sem("w_hi_done"), i + 1)
                pc = slice(i * PIECE, (i + 1) * PIECE)
                lo(w_lo[0][:, pc], wraw[:, pc], w_hi[0][:, pc], "w_lo_done")
            dve.wait_ge(sem("wr_hi_done"), 1)
            lo(wr_lo[:], wr_raw[:], wr_hi[:], "wr_lo_done")
            for c in range(NC):
                dve.wait_ge(sem("lg_done"), c + 1)
                dve.tensor_copy(logits[:, 4 * c:4 * c + 4],
                                b_v[c % 2][:].rearrange("p (t n) -> p t n", t=4)[:, :, 0:E]
                                ).then_inc(sem("lg_read"), 1)

            g_count = [0]

            def g(ins):
                g_count[0] += 1
                ins.then_inc(sem("g_done"), 1)
                dve.wait_ge(sem("g_done"), g_count[0])

            def per_expert(a):
                return a.unsqueeze(2).to_broadcast([P, TT, E])

            def gate_math():
                dve.wait_ge(sem("lg_read"), NC)
                ranks = rank[:].unsqueeze(1).to_broadcast([P, TT, E])
                for src, mx, sel, i in ((logits, g_m1, sel1, 0), (g_l2, g_m2, sel2, 1)):
                    g(dve.tensor_reduce(mx[:], src[:], AX.X, ALU.max))
                    g(dve.tensor_tensor(g_eq[:], src[:], per_expert(mx[:]), ALU.is_equal))
                    g(dve.tensor_tensor(g_w[:], g_eq[:], ranks, ALU.mult))
                    g(dve.tensor_reduce(g_r[:, i], g_w[:], AX.X, ALU.max))
                    g(dve.tensor_tensor(sel[:], g_w[:], per_expert(g_r[:, i]), ALU.is_equal))
                    if i == 0:
                        g(dve.scalar_tensor_tensor(out=g_l2[:], in0=sel1[:], scalar=-3e38, in1=logits[:],
                                                   op0=ALU.mult, op1=ALU.add))
                dve.tensor_tensor(g_d[:], g_m2[:], g_m1[:], ALU.subtract).then_inc(sem("g_diff"), 1)
                dve.wait_ge(sem("g_exp"), 1)
                g(dve.tensor_scalar(g_den[:], g_e[:], 1.0, None, ALU.add))
                g(dve.reciprocal(g_1[:], g_den[:]))
                g(dve.tensor_tensor(g_2[:], g_e[:], g_1[:], ALU.mult))
                g(dve.tensor_tensor(sel1[:], sel1[:], per_expert(g_1[:]), ALU.mult))
                g(dve.tensor_tensor(sel2[:], sel2[:], per_expert(g_2[:]), ALU.mult))
                g(dve.tensor_tensor(gates[:], sel1[:], sel2[:], ALU.add))

            def hidden(n, m, before):
                w = MT[m]
                dve.wait_ge(sem("silu_done"), 3 * n + m + 1)
                if before:
                    dve.wait_ge(sem("h_hi_done"), 3 * (n - 1) + m + 1)
                    dve.wait_ge(sem("h_lo_done"), 3 * (n - 1) + m + 1)
                dve.tensor_tensor(h32[0:w, m], b_v[m][0:w, :], silu[0:w, m], ALU.mult).then_inc(sem("h32_done"), 1)

            def hidden_low(n, m):
                w = MT[m]
                dve.wait_ge(sem("h_hi_done"), 3 * n + m + 1)
                dve.wait_ge(sem("h32_done"), 3 * n + m + 1)
                lo(h_lo[0:w, m], h32[0:w, m], h_hi[0:w, m], "h_lo_done")

            def add_y(n, c, e):
                for j in range(2):
                    dve.wait_ge(sem("y_done"), 2 * n + j + 1)
                    if isinstance(e, int) and e == 0:
                        a = acc[:, bass.ds(4 * c + 2 * j, 2)]
                        dve.tensor_tensor(a, b_y[j][:].rearrange("p (t n) -> p t n", t=2), a, ALU.add
                                          ).then_inc(sem("y_added"), 1)
                        continue
                    dve.wait_ge(sem("y_added"), 2 * n + j - 1)
                    for t in range(2):
                        tile = 4 * c + 2 * j + t
                        a = acc[:, bass.ds(tile, 1)].rearrange("p a n -> p (a n)")
                        gt = gates[:, bass.ds(tile, 1), bass.ds(e - 1, 1)].rearrange("p a b -> p (a b)")
                        ins = dve.scalar_tensor_tensor(out=a, in0=b_y[j][:, t * D:(t + 1) * D], scalar=gt, in1=a,
                                                       op0=ALU.mult, op1=ALU.add)
                    ins.then_inc(sem("y_added"), 1)

            def split_piece(e, c, par):
                dve.wait_ge(sem("w_hi_done"), PIECES * (e + 1) + c)
                pc = bass.ds((c - 1) * PIECE, PIECE)
                lo(w_lo[par][:, pc], wraw[:, pc], w_hi[par][:, pc], "w_lo_done")

            def norm_stats(c):
                dve.wait_ge(sem("y_added"), 2 * (NC * E + c) + 2)
                if above_zero(4 * c):
                    dve.wait_ge(sem("out_ready"), 4 * c)
                    dve.wait_ge(sem("bst2_done"), 4 * c)
                hold_dve(11)
                for t in range(4):
                    a = acc[:, bass.ds(4 * c + t, 1)].rearrange("p a n -> p (a n)")
                    dve.bn_stats(bst2[:, t], a).then_inc(sem("bst2_done"), 1)
                for t in range(4):
                    dve.wait_ge(sem("bst2_done"), 4 * c + t + 1)
                    if above_zero(4 * c + t):
                        dve.wait_ge(sem("mv2_done"), 4 * c + t)
                    hold_dve(12)
                    dve.bn_aggr(mv2[:, t], bst2[:, t]).then_inc(sem("mv2_done"), 1)

            def chunk(e, c, par, before, before_e=None, last=False):
                n = NC * e + c
                hidden(n, 0, before)
                if before:
                    if before_e is None:
                        add_y(n - 1, c - 1, e)
                    else:
                        add_y(n - 1, NC - 1, before_e)
                hidden_low(n, 0)
                for m in (1, 2):
                    hidden(n, m, before)
                    hidden_low(n, m)
                if before_e is None and before and not last:
                    split_piece(e, c, 1 - par)
                if before_e is None and before and last:
                    norm_stats(c - 1)

            def expert(e, par, last=False):
                chunk(e, 0, par, True, before_e=e - 1)
                if last:
                    chunk(e, 1, par, True, last=True)
                with dve.Fori(2 if last else 1, NC) as c:
                    chunk(e, c, par, True, last=last)

            chunk(0, 0, 0, False)
            gate_math()
            dve.wait_ge(sem("acc0_loaded"), 16)
            chunk(0, 1, 0, True)
            dve.wait_ge(sem("acc_loaded"), 16)
            with dve.Fori(2, NC) as c:
                chunk(0, c, 0, True)
            n1 = NC
            hidden(n1, 0, True)
            add_y(n1 - 1, NC - 1, 0)
            hidden_low(n1, 0)
            for m in (1, 2):
                hidden(n1, m, True)
                hidden_low(n1, m)
            with dve.Fori(1, NC) as c:
                chunk(1, c, 1, True)
            with dve.Fori(1, E // 2) as j:
                expert(2 * j, 0)
                expert(2 * j + 1, 1)
            expert(E, 0, last=True)
            add_y(NC * (E + 1) - 1, NC - 1, E)
            norm_stats(NC - 1)

        @block.gpsimd
        def _(pool):
            def hi(out_ap, in_ap, name):
                pool.tensor_scalar(out_ap, in_ap, 1.0, 0.0, ALU.mult, ALU.add).then_inc(sem(name), 1)

            def x_high(b):
                pool.wait_ge(sem("xT_loaded"), 16 * (b + 1))
                if above_zero(2 * b):
                    pool.wait_ge(sem("down_done"), 2 * b)
                if above_zero(b):
                    pool.wait_ge(sem("xhi_done"), b)
                hold_pool(0)
                hi(x_hi[:], x_raw[:], "xhi_done")

            def inv_rms(b, t):
                idx = 2 * b + t
                pool.wait_ge(sem("ss_done"), 2 * idx + 2)
                if above_zero(2 * (idx - 1)):
                    pool.wait_ge(sem("an_done"), 2 * (idx - 1))
                if above_zero(idx):
                    pool.wait_ge(sem("ms_done"), idx)
                hold_pool(1)
                pool.tensor_scalar(ms[:, t], ss[:, t], 1.0, RMS_EPS, ALU.mult, ALU.add).then_inc(sem("ms_done"), 1)
                pool.wait_ge(sem("ms_done"), idx + 1)
                pool.tensor_tensor(rstd[:, t], ms[:, t], mhalf[:], ALU.pow).then_inc(sem("rstd_done"), 1)

            def k_high(b, t, par):
                tt = slice(t * P, (t + 1) * P)
                pool.wait_ge(sem("kT_done"), 2 * b + t + 1)
                if above_zero(BATCH_STEPS * (b - 1)):
                    pool.wait_ge(sem("s_done"), BATCH_STEPS * (b - 1))
                if above_zero(2 * b + t):
                    pool.wait_ge(sem("k_hi_done"), 2 * b + t)
                hold_pool(2)
                hi(k_hi[par][:, tt], kT[par][:, tt], "k_hi_done")

            def values(b, par):
                pool.wait_ge(sem("an_done"), 2 * (2 * b + 2))
                if above_zero(BATCH_STEPS * (b - 1)):
                    pool.wait_ge(sem("ctx_done"), BATCH_STEPS * (b - 1))
                if above_zero(b):
                    pool.wait_ge(sem("v1_done"), b)
                hold_pool(3)
                hi(v0_hi[par][:, KL:2 * KL], an[:, 0, QL:QL + KL], "v0_hi_done")
                hi(v1[par][:, KL:2 * KL], an[:, 1, QL:QL + KL], "v1_done")

            pool.memset(held_in[:], 0.0).then_inc(sem("held_set"), 1)
            pool.wait_ge(sem("held_set"), 1)
            pool.wait_ge(sem("wa_loaded"), 16)
            hi(wa_hi[:], wa_raw[:], "wa_hi_done")
            x_high(0)
            pool.memset(mhalf[:], -0.5).then_inc(sem("mhalf_set"), 1)
            pool.wait_ge(sem("mhalf_set"), 1)
            pool.memset(ident[:], 0.0).then_inc(sem("pool_set"), 1)
            pool.memset(mask[:], 0.0).then_inc(sem("pool_set"), 1)
            for i in range(2):
                for j in (slice(0, KL), slice(2 * KL, 3 * KL)):
                    pool.memset(v0_hi[i][:, j].bitcast(F32), 0.0)
                    pool.memset(v0_lo[i][:, j].bitcast(F32), 0.0)
                    ins = pool.memset(v1[i][:, j], 0.0)
            ins.then_inc(sem("pads_done"), 1)
            pool.wait_ge(sem("pool_set"), 2)
            pool.affine_select(out=ident[:], in_=ident[:], compare_op=ALU.not_equal, fill=1.0, base=0,
                               pattern=[[-1, P]], channel_multiplier=1).then_inc(sem("ident_done"), 1)
            pool.affine_select(out=mask[:, P:S], in_=mask[:, P:S], compare_op=ALU.is_ge, fill=MASKED, base=0,
                               pattern=[[-1, P]], channel_multiplier=1).then_inc(sem("mask_done"), 1)
            pool.wait_ge(sem("pads_done"), 1)
            for t in range(2):
                inv_rms(0, t)
                k_high(0, t, 0)
            values(0, 0)

            def step(B, u, first, last, tail):
                s = BODY * B + u
                b, p = batch_of(B, u)
                nx = has_next(u, last, tail)
                npar = (u // BATCH_STEPS + 1) % 2
                if p == 0 and nx:
                    x_high(b + 1)
                if live(u, LAG_SM, first, tail):
                    q, i = s - LAG_SM, (u - LAG_SM) % 2
                    pool.wait_ge(sem("rden_done"), q + 1)
                    if above_zero(4 * q):
                        pool.wait_ge(sem("norm_done"), 4 * q)
                    hold_pool(4)
                    for h in range(2):
                        for t in range(2):
                            cols = slice(0, P) if t == 0 else slice(P, 3 * P)
                            z = 2 * h + t
                            pool.tensor_scalar(probs[i][:, h, cols], probs[i][:, h, cols], rden[i][:, z:z + 1], 1.0,
                                               ALU.mult, ALU.mult).then_inc(sem("norm_done"), 1)
                if not tail:
                    t, qp = u % 2, (u // 2) % 2
                    pool.wait_ge(sem("rope_done"), s + 1)
                    if not (first and u < 4):
                        pool.wait_ge(sem("qTb_done"), s - t - 2)
                    pool.tensor_tensor(q_nat[qp][t][:, :, KL:P], r1[:], r2[:], ALU.add).then_inc(sem("qrope_done"), 1)
                if p in (2, 4) and nx:
                    inv_rms(b + 1, p // 2 - 1)
                if p in (3, 5) and nx:
                    k_high(b + 1, p // 2 - 1, npar)
                if p == 6 and nx:
                    values(b + 1, npar)
                if p == 5 and has_prev(u, first):
                    pool.wait_ge(sem("mv_done"), 2 * b)
                    if above_zero(2 * (b - 1)):
                        pool.wait_ge(sem("ln_done"), 2 * (b - 1))
                    if above_zero(b - 1):
                        pool.wait_ge(sem("vps_done"), b - 1)
                    hold_pool(5)
                    pool.tensor_scalar(vps[:], mv[:, :, 1], 1.0, LN_EPS, ALU.mult, ALU.add
                                       ).then_inc(sem("vps_done"), 1)
                    pool.wait_ge(sem("vps_done"), b)
                    pool.tensor_tensor(lnr[:], vps[:], mhalf[:], ALU.pow).then_inc(sem("lnr_done"), 1)

            bodies(pool, step)

            pool.wait_ge(sem("x1t_lo"), NB)
            pool.wait_ge(sem("x1_stored"), 16 * NB)
            pool.wait_ge(sem("wraw_loaded"), 16)
            for i in range(PIECES):
                hi(w_hi[0][:, i * PIECE:(i + 1) * PIECE], wraw[:, i * PIECE:(i + 1) * PIECE], "w_hi_done")
            pool.dma_start(wr_raw[:], wrT.rearrange("(k p) n -> p k n", p=P)).then_inc(sem("wr_loaded"), 16)
            for e in range(E):
                ins = pool.memset(rank[:, e:e + 1], float(E - e))
            pool.memset(mhalf4[:], -0.5).then_inc(sem("rank_done"), 1)
            pool.wait_ge(sem("wr_loaded"), 16)
            hi(wr_hi[:], wr_raw[:], "wr_hi_done")

            def inv_std(c):
                pool.wait_ge(sem("mv2_done"), 4 * c + 4)
                if above_zero(4 * c):
                    pool.wait_ge(sem("out_ready"), 4 * c)
                if above_zero(c):
                    pool.wait_ge(sem("vps2"), c)
                hold_pool(6)
                pool.tensor_scalar(vps2[:], mv2[:, :, 1], 1.0, LN_EPS, ALU.mult, ALU.add).then_inc(sem("vps2"), 1)
                pool.wait_ge(sem("vps2"), c + 1)
                pool.tensor_tensor(rs2[:], vps2[:], mhalf4[:], ALU.pow).then_inc(sem("rs2_done"), 1)
                pool.wait_ge(sem("rs2_done"), c + 1)
                pool.tensor_tensor(mr2[:], mv2[:, :, 0], rs2[:], ALU.mult).then_inc(sem("mr2_done"), 1)
                pool.wait_ge(sem("mr2_done"), c + 1)
                if above_zero(c):
                    pool.wait_ge(sem("ln2_done"), c)
                hold_pool(7)
                pool.tensor_scalar(nb2[:], mr2[:], -1.0, 0.0, ALU.mult, ALU.add).then_inc(sem("ln2_done"), 1)

            inv_std(0)
            with pool.Fori(1, NC) as c:
                inv_std(c)


def kernel(**inputs):
    import numpy as np
    import concourse.bacc as bacc
    from concourse.bass_utils import run_bass_kernel_spmd

    g = {k: np.asarray(v) for k, v in inputs.items()}
    x = g["L0_attn_hidden_states"]

    def t(a):
        return np.ascontiguousarray(np.swapaxes(a, -1, -2))

    wffn = np.zeros((E + 1, P, WCOLS), np.float32)
    for e in range(E + 1):
        w1, w2, w3 = ((g["L0_ffn_sw1"], g["L0_ffn_sw2"], g["L0_ffn_sw3"]) if e == 0 else
                      (g["L0_ffn_ew1"][e - 1], g["L0_ffn_ew2"][e - 1], g["L0_ffn_ew3"][e - 1]))
        for k in range(2):
            wffn[e, :, k * HF:(k + 1) * HF] = w1.T[k * P:(k + 1) * P]
            wffn[e, :, W3_AT + k * HF:W3_AT + (k + 1) * HF] = w3.T[k * P:(k + 1) * P]
        for k, rows in enumerate(MT):
            wffn[e, :rows, W2_AT + k * D:W2_AT + (k + 1) * D] = w2.T[k * P:k * P + rows]
    wrT = np.zeros((D, P), np.float32)
    wrT[:, :E] = g["L0_ffn_wr"].T
    inv_freq = (1.0 / np.float32(10000.0) ** (np.arange(0, DR, 2, dtype=np.float32) / np.float32(DR))
                ).astype(np.float32)
    fr = np.outer(np.arange(S, dtype=np.float32), inv_freq).astype(np.float32)
    rope = np.stack([np.concatenate([np.cos(fr), np.cos(fr)], -1),
                     np.concatenate([-np.sin(fr), np.sin(fr)], -1)]).astype(np.float32)
    arrays = {
        "x_in": x, "xT_in": t(x),
        "waT_in": np.ascontiguousarray(np.concatenate([g["L0_attn_w_qa"], g["L0_attn_w_kva"]], 0).T),
        "wqb_in": g["L0_attn_w_qb"], "wqbT_in": t(g["L0_attn_w_qb"]), "wkvb_in": g["L0_attn_w_kvb"],
        "woT_in": t(g["L0_attn_w_o"]), "aln_in": g["L0_attn_q_a_ln_w"], "kvln_in": g["L0_attn_kv_a_ln_w"],
        "rope_in": rope, "wrT_in": wrT, "wffn_in": wffn,
    }
    nc = bacc.Bacc("TRN2", target_bir_lowering=False, num_devices=1)
    args = [nc.dram_tensor(k, a.shape, F32, kind="ExternalInput").ap() for k, a in arrays.items()]
    args.append(nc.dram_tensor("x1_scratch", x.shape, F32, kind="Internal").ap())
    args.append(nc.dram_tensor("out_dram", x.shape, F32, kind="ExternalOutput").ap())
    build(nc, *args)
    r = run_bass_kernel_spmd(nc, [arrays], core_ids=[0])
    return r.results[0]["out_dram"]
```

```python
from contextlib import ExitStack

import concourse.bass as bass
from concourse import mybir

F32 = mybir.dt.float32
F32R = mybir.dt.float32r
BF16 = mybir.dt.bfloat16
I32 = mybir.dt.int32
U32 = mybir.dt.uint32
ALU = mybir.AluOpType
ACT = mybir.ActivationFunctionType
AX = mybir.AxisListType

P = 128
NB, S, D = 16, 256, 256
H, QL, KL = 16, 192, 64
DN, DR, DV = 128, 64, 128
DQ = DN + DR
NA = QL + KL + DR
HI = QL - P
CKV = QL + HI
SCALE = float(DQ) ** -0.5
RMS_EPS, LN_EPS = 1e-6, 1e-5
MASKED = -1e30
PAIRS = H // 2
TT = NB * S // P
BATCH_STEPS = PAIRS
BODY = 2 * BATCH_STEPS
LAG_QT, LAG_SC, LAG_SM, LAG_PV, LAG_WO = 2, 3, 4, 5, 6

E = 8
HF = 4 * D // 3
MT = [128, 128, HF - 256]
C = 512
NC = NB * S // C
NJ = (2 * NB * S + E * (C - 1)) // C
NU = NJ + NC
REGION = NB * S
W3_AT = 2 * HF
W13, W2 = 4 * HF, 3 * D
ROUTE_OPS = 18
SLOTS = {1: (0, 7), 2: (7, 13), 4: (13, 18)}
T_RANK, T_REGION, T_THR, T_EIDX, T_LTRI, T_J1, T_TP, T_P = 0, 8, 16, 24, 32, 96, 96 + NJ, 100 + NJ
T_COLS = T_P + 1


def build(nc, x, xT, waT, wqb, wqbT, wkvb, woT, aln, kvln, rope, wrT, w13_all, w2_all, table, mats,
          x1_dram, x_sorted, y_sorted, out):
    with ExitStack() as top:
        names = {}

        def sb(stack, name, shape, dt=F32):
            return stack.enter_context(nc.sbuf_tensor(name, shape, dt))

        def bank(name):
            return top.enter_context(nc.psum_tensor(name, [P, 512], F32))

        def sem(name):
            if name not in names:
                names[name] = top.enter_context(nc.semaphore(name))
            return names[name]

        ident = sb(top, "ident", [P, P])
        held = sb(top, "held", [P, 16])
        held_in = sb(top, "held_in", [P, 1])
        w13_raw = sb(top, "w13_raw", [P, W13])
        w2_raw = sb(top, "w2_raw", [P, W2])
        xs = [sb(top, f"xs{i}", [P, 2, D]) for i in range(2)]
        tab = sb(top, "tab", [P, T_COLS])
        tri = sb(top, "tri", [P, P])
        ones = sb(top, "ones", [P, P])
        tri_b = sb(top, "tri_b", [P, P], BF16)
        ones_b = sb(top, "ones_b", [P, P], BF16)
        zeros = sb(top, "zeros", [P, 2 * D])
        wr32 = sb(top, "wr32", [P, 2, E])
        xt32 = sb(top, "xt32", [P, 2, S])
        lg = sb(top, "lg", [P, 2, E])
        lg2 = sb(top, "lg2", [P, 2, E])
        r_m = sb(top, "r_m", [P, 2, 2])
        r_eq = sb(top, "r_eq", [P, 2, E])
        r_w = sb(top, "r_w", [P, 2, E])
        r_r = sb(top, "r_r", [P, 2, 2])
        sel = sb(top, "sel", [P, 2, 2, E])
        picked = sb(top, "picked", [P, 2, E], BF16)
        pfx = sb(top, "pfx", [P, 3, E])
        run = [sb(top, f"run{i}", [P, E]) for i in range(2)]
        posf = sb(top, "posf", [P, 2, E])
        posw = sb(top, "posw", [P, 2, 2, E])
        stash = [sb(top, f"stash{i}", [P, 6]) for i in range(2)]
        pos_i = [sb(top, f"pos_i{i}", [P, 4], I32) for i in range(2)]
        stash_all = sb(top, "stash_all", [P, NB, 6])
        with ExitStack() as staging:
            wa_raw = sb(staging, "wa_raw", [P, 2, NA])
            wq_nope = sb(staging, "wq_nope", [P, H, QL])
            wk_nat = sb(staging, "wk_nat", [P, H, KL])
            wv_nat = sb(staging, "wv_nat", [P, H, KL])
            wo_t = sb(staging, "wo_t", [P, H, D])
            wq_pe = sb(staging, "wq_pe", [P, 2, H, DR])
        xg = [sb(top, f"xg{i}", [P, 4, D]) for i in range(2)]
        xh = [sb(top, f"xh{i}", [P, 2, C], F32R) for i in range(2)]
        xl = [sb(top, f"xl{i}", [P, 2, C], F32R) for i in range(2)]
        w13_hi = [sb(top, "w13_hi0", [P, W13], F32R)]
        w13_lo = [sb(top, "w13_lo0", [P, W13], F32R)]
        w2_hi = [sb(top, "w2_hi0", [P, W2], F32R)]
        w2_lo = [sb(top, "w2_lo0", [P, W2], F32R)]
        ys = [sb(top, f"ys{i}", [P, 4, D]) for i in range(2)]

        with ExitStack() as att:
            wa_hi = sb(att, "wa_hi", [P, 2, NA], F32R)
            wa_lo = sb(att, "wa_lo", [P, 2, NA], F32R)
            m_hi = sb(att, "m_hi", [P, 2, H, P], F32R)
            m_lo = sb(att, "m_lo", [P, 2, H, P], F32R)
            wvo_hi = sb(att, "wvo_hi", [P, PAIRS, D], F32R)
            wvo_lo = sb(att, "wvo_lo", [P, PAIRS, D], F32R)
            aln_c = sb(att, "aln_c", [P, 2])
            kvln2 = sb(att, "kvln2", [P, 1])
            kvln1 = sb(att, "kvln1", [P, 1])
            cos = sb(att, "cos", [P, 2, DR])
            sgn = sb(att, "sgn", [P, 2, DR])
            mask = sb(att, "mask", [P, S])
            mhalf = sb(att, "mhalf", [P, 2])
            x_raw = sb(att, "x_raw", [P, 2, S])
            x_hi = sb(att, "x_hi", [P, 2, S], F32R)
            x_lo = sb(att, "x_lo", [P, 2, S], F32R)
            x_nat = sb(att, "x_nat", [P, 2, D])
            sq = sb(att, "sq", [P, QL])
            ss = sb(att, "ss", [P, 2, 2])
            ms = sb(att, "ms", [P, 2, 2])
            rstd = sb(att, "rstd", [P, 2, 2])
            kr1 = sb(att, "kr1", [P, DR])
            kr2 = sb(att, "kr2", [P, DR])
            an = sb(att, "an", [P, 2, NA + HI])
            cq_hi = [sb(att, f"cq_hi{i}", [P, 2, S], F32R) for i in range(2)]
            cq_lo = [sb(att, f"cq_lo{i}", [P, S], F32R) for i in range(2)]
            kT = [sb(att, f"kT{i}", [P, S]) for i in range(2)]
            k_hi = [sb(att, f"k_hi{i}", [P, S], F32R) for i in range(2)]
            k_lo = [sb(att, f"k_lo{i}", [P, S], F32R) for i in range(2)]
            v0_hi = [sb(att, f"v0_hi{i}", [P, 3 * KL], F32R) for i in range(2)]
            v0_lo = [sb(att, f"v0_lo{i}", [P, 3 * KL], F32R) for i in range(2)]
            v1 = [sb(att, f"v1_{i}", [P, 3 * KL]) for i in range(2)]
            q_nat = [[sb(att, f"q_nat{i}{t}", [P, 4, P]) for t in range(2)] for i in range(2)]
            r1 = sb(att, "r1", [P, 4, DR])
            r2 = sb(att, "r2", [P, 4, DR])
            qT = [sb(att, f"qT{i}", [P, 2, P]) for i in range(2)]
            qT_hi = [sb(att, f"qT_hi{i}", [P, 2, P], F32R) for i in range(2)]
            qT_lo = [sb(att, f"qT_lo{i}", [P, 2, P], F32R) for i in range(2)]
            probs = [sb(att, f"probs{i}", [P, 2, 3 * P]) for i in range(2)]
            negmax = [sb(att, f"negmax{i}", [P, 4]) for i in range(2)]
            psums = [sb(att, f"psums{i}", [P, 4]) for i in range(2)]
            rden = [sb(att, f"rden{i}", [P, 4]) for i in range(2)]
            pT_hi = sb(att, "pT_hi", [P, 2, S], F32R)
            pT_lo = sb(att, "pT_lo", [P, 2, S], F32R)
            pT_k1 = sb(att, "pT_k1", [P, 2, P])
            ctx_hi = [sb(att, f"ctx_hi{i}", [P, S], F32R) for i in range(2)]
            ctx_lo = [sb(att, f"ctx_lo{i}", [P, S], F32R) for i in range(2)]
            bst = sb(att, "bst", [P, 2, 6])
            mv = sb(att, "mv", [P, 2, 2])
            vps = sb(att, "vps", [P, 2])
            lnr = sb(att, "lnr", [P, 2])

        ffn = top
        w13_hi.append(sb(ffn, "w13_hi1", [P, W13], F32R))
        w13_lo.append(sb(ffn, "w13_lo1", [P, W13], F32R))
        w2_hi.append(sb(ffn, "w2_hi1", [P, W2], F32R))
        w2_lo.append(sb(ffn, "w2_lo1", [P, W2], F32R))
        acc = sb(ffn, "acc", [P, TT, D])
        silu = sb(ffn, "silu", [P, 3, C])
        h32 = sb(ffn, "h32", [P, 3, C])
        h_hi = sb(ffn, "h_hi", [P, 3, C], F32R)
        h_lo = sb(ffn, "h_lo", [P, 3, C], F32R)
        yg = [sb(ffn, f"yg{i}", [P, 2, 4, D]) for i in range(2)]
        t_n = sb(ffn, "t_n", [P, E])
        t_cmp = sb(ffn, "t_cmp", [P, E, E])
        t_nb = sb(ffn, "t_nb", [P, E])
        t_cum = sb(ffn, "t_cum", [P, E, E])
        t_end = sb(ffn, "t_end", [P, E])
        t_start = sb(ffn, "t_start", [P, E])
        t_j = sb(ffn, "t_j", [P, NJ])
        t_ge = sb(ffn, "t_ge", [P, NJ, E])
        t_lt = sb(ffn, "t_lt", [P, NJ, E])
        t_oh = sb(ffn, "t_oh", [P, NJ, E])
        t_w = sb(ffn, "t_w", [P, 3, NJ, E])
        t_sum = sb(ffn, "t_sum", [P, 3, NJ])
        t_k0 = sb(ffn, "t_k0", [P, NJ])
        t_k1 = sb(ffn, "t_k1", [P, NJ])
        t_k = sb(ffn, "t_k", [P, NJ, 4])
        t_last = sb(ffn, "t_last", [P, NJ])
        t_km = sb(ffn, "t_km", [P, NJ, 4])
        t_base = sb(ffn, "t_base", [P, NJ])
        t_row = sb(ffn, "t_row", [P, NJ, 4])
        t_wrow = sb(ffn, "t_wrow", [P, NJ])
        row_i = sb(ffn, "row_i", [P, NJ, 4], I32)
        wrow_i = sb(ffn, "wrow_i", [P, NJ], I32)
        t_s512 = sb(ffn, "t_s512", [P, E])
        t_delta = sb(ffn, "t_delta", [P, E + 1])
        t_dd = sb(ffn, "t_dd", [P, E])
        t_in = sb(ffn, "t_in", [P, NB, 4, E])
        t_inw = sb(ffn, "t_inw", [P, NB, 4, E])
        t_shift = sb(ffn, "t_shift", [P, NB, 4])
        t_y = sb(ffn, "t_y", [P, NB, 4])
        yrow_i = sb(ffn, "yrow_i", [P, NB, 4], I32)
        g_e = sb(ffn, "g_e", [P, NB, 2])
        g_den = sb(ffn, "g_den", [P, NB, 2])
        g_1 = sb(ffn, "g_1", [P, NB * 2])
        g_2 = sb(ffn, "g_2", [P, NB * 2])
        mhalf4 = sb(ffn, "mhalf4", [P, 4])
        bst2 = sb(ffn, "bst2", [P, 4, 6])
        mv2 = sb(ffn, "mv2", [P, 4, 2])
        vps2 = sb(ffn, "vps2", [P, 4])
        rs2 = sb(ffn, "rs2", [P, 4])
        mr2 = sb(ffn, "mr2", [P, 4])
        nb2 = sb(ffn, "nb2", [P, 4])

        b_q = bank("b_q")
        b_qT = bank("b_qT")
        b_s = [bank("b_s0"), bank("b_s1")]
        b_pT = bank("b_pT")
        b_c = bank("b_c")
        b_o = bank("b_o")
        b_x = bank("b_x")
        b_u, b_v, b_y = [b_q, b_qT, b_s[0]], [b_s[1], b_pT, b_c], [b_o, b_x]

        def live(u, lag, first, tail):
            return (not first or u >= lag) and (not tail or u < lag)

        def bodies(engine, step, tail_steps=BATCH_STEPS):
            for B in range(2):
                for u in range(BODY):
                    step(B, u, B == 0, False, False)
            with engine.Fori(2, NB // 2 - 1) as B:
                for u in range(BODY):
                    step(B, u, False, False, False)
            for u in range(BODY):
                step(NB // 2 - 1, u, False, True, False)
            for u in range(tail_steps):
                step(NB // 2, u, False, False, True)

        def batch_of(B, u):
            return 2 * B + u // BATCH_STEPS, u % BATCH_STEPS

        def has_next(u, last, tail):
            return not tail and not (last and u >= BATCH_STEPS)

        def has_prev(u, first):
            return not (first and u < BATCH_STEPS)

        def above_zero(count):
            return not isinstance(count, int) or count > 0

        def hold_dve(column):
            return nc.vector.memset(held[:, column:column + 1], 0.0)

        def hold_pool(column):
            return nc.gpsimd.tensor_tensor(held[:, column:column + 1], held_in[:], held_in[:], ALU.add)

        block = top.enter_context(nc.Block())

        @block.sync
        def _(sp):
            sp.dma_start(x_raw[:], xT[0].rearrange("(k p) n -> p k n", p=P)).then_inc(sem("xT_loaded"), 16)
            sp.dma_start(wa_raw[:], waT.rearrange("(k p) n -> p k n", p=P)).then_inc(sem("wa_loaded"), 16)
            for i in range(2):
                sp.dma_start(cos[:, i], rope[0, i * P:(i + 1) * P]).then_inc(sem("rope_loaded"), 16)
                sp.dma_start(sgn[:, i], rope[1, i * P:(i + 1) * P]).then_inc(sem("rope_loaded"), 16)
            sp.dma_start(wq_nope[:], wqb.rearrange("(h c) r -> c h r", h=H)[0:DN]).then_inc(sem("wq_loaded"), 16)
            sp.dma_start(wq_pe[:, 0], wqbT.rearrange("r (h c) -> r h c", h=H)[0:P, :, DN:DQ]
                         ).then_inc(sem("wpe_loaded"), 16)
            for rows in (slice(0, HI), slice(HI, 2 * HI)):
                sp.dma_start(wq_pe[rows, 1], wqbT.rearrange("r (h c) -> r h c", h=H)[P:QL, :, DN:DQ]
                             ).then_inc(sem("wpe_loaded"), 16)
            sp.dma_start(wo_t[:], woT.rearrange("(h p) n -> p h n", p=P)).then_inc(sem("wo_loaded"), 16)
            sp.dma_start(tab[:], table).then_inc(sem("tab_loaded"), 16)
            sp.dma_start(tri[:], mats[0]).then_inc(sem("tab_loaded"), 16)
            sp.dma_start(ones[:], mats[1]).then_inc(sem("tab_loaded"), 16)
            with nc.allow_non_contiguous_dma(reason="the router's weights, eight columns"):
                sp.dma_start(wr32[:], wrT.rearrange("(k p) n -> p k n", p=P)).then_inc(sem("tab_loaded"), 16)

            def batch(b, par, head, rest):
                following = b + 1
                if rest:
                    sp.wait_ge(sem("xhi_done"), following)
                    sp.wait_ge(sem("xlo_done"), following)
                    sp.dma_start(x_raw[:], xT[following].rearrange("(k p) n -> p k n", p=P)
                                 ).then_inc(sem("xT_loaded"), 16)
                if not head:
                    store_x1(b - 1, 1 - par)
                    sp.wait_ge(sem("ln_r"), b)
                sp.dma_start(x_nat[:], x[b].rearrange("(t p) n -> p t n", p=P)).then_inc(sem("xnat_loaded"), 16)

            def store_x1(b, par):
                sp.wait_ge(sem("ln_done"), 2 * (b + 1))
                sp.dma_start(x1_dram[b].rearrange("(t p) n -> p t n", p=P), xs[par][:]
                             ).then_inc(sem(f"x1_stored{par}"), 16)

            batch(0, 0, True, True)
            with sp.Fori(0, NB // 2 - 1) as j:
                batch(2 * j + 1, 1, False, True)
                batch(2 * j + 2, 0, False, True)
            batch(NB - 1, 1, False, False)
            x1_v = x1_dram.rearrange("b (t p) n -> p (b t) n", p=P)
            store_x1(NB - 1, 1)

            sp.wait_ge(sem("x1_stored1"), 16 * (NB // 2))
            sp.dma_start(acc[:], x1_v).then_inc(sem("acc_loaded"), 16)

            def store_y(j, par):
                sp.wait_ge(sem("y_copied"), 2 * j + 2)
                sp.dma_start(y_sorted[bass.ds(j * C, C)].rearrange("(t p) n -> p t n", p=P), ys[par][:]
                             ).then_inc(sem(f"y_stored{par}"), 16)

            store_y(0, 1)
            with sp.Fori(0, NJ // 2) as i:
                store_y(2 * i + 1, 0)
                store_y(2 * i + 2, 1)
            out_v = out.rearrange("b (t p) n -> p (b t) n", p=P)
            with sp.Fori(0, NC) as c:
                sp.wait_ge(sem("out_ready"), 4 * c + 4)
                sp.dma_start(out_v[:, bass.ds(4 * c, 4)], acc[:, bass.ds(4 * c, 4)]).then_inc(sem("out_stored"), 16)
            sp.wait_ge(sem("out_stored"), 16 * NC)

        @block.tensor
        def _(pe):
            def passes(out_ap, terms, start=True, stop=True, chk=False):
                for i, (w, m) in enumerate(terms):
                    mm = pe.matmul(out_ap, w, m, start=start and i == 0, stop=stop and i == len(terms) - 1,
                                   skip_group_check=chk)
                return mm

            def split3(w, m):
                return [(w[0], m[0]), (w[1], m[0]), (w[0], m[1])]

            def down(b, t):
                idx = 2 * b + t
                pe.wait_ge(sem("xhi_done"), b + 1)
                pe.wait_ge(sem("xlo_done"), b + 1)
                if t == 0:
                    if above_zero(b - 2):
                        pe.wait_ge(sem("x1t_read"), b - 2)
                else:
                    pe.wait_ge(sem("cq_hi_done"), idx)
                    pe.wait_ge(sem("cq_lo_done"), idx)
                    pe.wait_ge(sem("kT_done"), idx)
                tt = slice(t * P, (t + 1) * P)
                terms = [z for k in range(2) for z in split3((x_hi[:, k, tt], x_lo[:, k, tt]),
                                                             (wa_hi[:, k], wa_lo[:, k]))]
                passes(b_x[:, 0:NA], terms).then_inc(sem("down_done"), 1)

            def down_T(b, t):
                idx = 2 * b + t
                pe.wait_ge(sem("an_done"), 3 * idx + 3)
                pe.wait_ge(sem("kpe_done"), idx + 1)
                pe.transpose(b_x[:, 0:P], an[:, t, 0:P], ident[:])
                pe.transpose(b_x[:, P:2 * P], an[:, t, P:2 * P], ident[:])
                pe.transpose(b_x[:, 2 * P:3 * P], an[:, t, 2 * P:3 * P], ident[:]).then_inc(sem("downT_done"), 1)

            def x1_T(b, par):
                pe.wait_ge(sem("ln_done"), 2 * (b + 1))
                for k in range(2):
                    for t in range(2):
                        mm = pe.transpose(b_x[:, (2 * k + t) * P:(2 * k + t + 1) * P],
                                          xs[par][:, t, k * P:(k + 1) * P], ident[:])
                mm.then_inc(sem("x1T_done"), 1)

            def router(r):
                pe.wait_ge(sem("x1t_read"), r + 1)
                for t in range(2):
                    for k in range(2):
                        mm = pe.matmul(b_s[0][:, 3 * P + t * E:3 * P + (t + 1) * E], xt32[:, k, t * P:(t + 1) * P],
                                       wr32[:, k], start=(k == 0), stop=(k == 1))
                mm.then_inc(sem("logits_done"), 1)

            def prefix(r):
                pe.wait_ge(sem("route_step"), ROUTE_OPS * r + 12)
                for i, terms in enumerate(([(tri_b, 0)], [(tri_b, 1), (ones_b, 0)],
                                           [(ones_b, 0), (ones_b, 1)])):
                    mm = passes(b_s[0][:, 3 * P + i * E:3 * P + (i + 1) * E],
                                [(m[:], picked[:, t]) for m, t in terms])
                mm.then_inc(sem("prefix_done"), 1)

            pe.wait_ge(sem("wa_hi_done"), 1)
            pe.wait_ge(sem("wa_lo_done"), 1)
            down(0, 0)
            pe.wait_ge(sem("wq_loaded"), 16)
            pe.wait_ge(sem("wkv_loaded"), 32)
            for k, rows in ((0, P), (1, QL - P)):
                for g in range(2):
                    dst = (b_q, b_qT, b_s[0], b_s[1])[2 * k + g]
                    for i in range(8):
                        h = 8 * g + i
                        for at in range(0, P, rows):
                            mm = pe.matmul(dst[at:at + rows, i * KL:(i + 1) * KL],
                                           wq_nope[:, h, k * P:k * P + rows], wk_nat[:, h], start=True, stop=True)
                    mm.then_inc(sem("wm_done"), 1)
            pe.wait_ge(sem("ident_done"), 1)
            down_T(0, 0)
            down(0, 1)
            pe.wait_ge(sem("wo_loaded"), 16)

            def value_out(g, dst):
                for i in range(2):
                    for hh in range(2):
                        h = 4 * g + 2 * i + hh
                        mm = pe.matmul(dst[hh * KL:(hh + 1) * KL, i * D:(i + 1) * D], wv_nat[:, h], wo_t[:, h],
                                       start=True, stop=True)
                mm.then_inc(sem("wvo_done"), 1)

            for g, dst in enumerate((b_pT, b_c, b_o)):
                value_out(g, dst)
            down_T(0, 1)
            pe.wait_ge(sem("cq_hi_done"), 2)
            pe.wait_ge(sem("cq_lo_done"), 2)
            pe.wait_ge(sem("kT_done"), 2)
            value_out(3, b_x)
            pe.wait_ge(sem("prep_hi"), 10)
            pe.wait_ge(sem("prep_lo"), 10)

            def step(B, u, first, last, tail):
                s = BODY * B + u
                b, p = batch_of(B, u)
                if live(u, LAG_PV, first, tail):
                    q = s - LAG_PV
                    pe.wait_ge(sem("norm_done"), 4 * q + 4)
                    if above_zero(q):
                        pe.wait_ge(sem("ctx_lo_done"), q)
                    pr = probs[(u - LAG_PV) % 2]
                    for h in range(2):
                        for t in range(2):
                            pe.transpose(b_pT[:, h * S + t * P:h * S + (t + 1) * P], pr[:, h, t * P:(t + 1) * P],
                                         ident[:])
                    for h in range(2):
                        mm = pe.transpose(b_c[:, h * P:(h + 1) * P], pr[:, h, 2 * P:3 * P], ident[:])
                    mm.then_inc(sem("pT_done"), 1)
                if not tail:
                    t, quad, par = u % 2, (u // 2) % 4, (u // BATCH_STEPS) % 2
                    if above_zero(s):
                        pe.wait_ge(sem("rope_done"), s)
                    if p == 0:
                        pe.wait_ge(sem("cq_hi_done"), 2 * b + 2)
                        pe.wait_ge(sem("cq_lo_done"), 2 * b + 2)
                    tt = slice(t * P, (t + 1) * P)
                    hs = slice(4 * quad, 4 * quad + 4)
                    terms = split3((cq_hi[par][:, 0, tt], cq_lo[par][:, tt]), (m_hi[:, 0, hs], m_lo[:, 0, hs]))
                    terms += [(cq_hi[par][:, 1, tt], m_hi[:, 1, hs]),
                              (cq_hi[par][0:HI, 1, tt], m_lo[0:HI, 1, hs])]
                    passes(b_q[:], terms).then_inc(sem("q_done"), 1)
                if live(u, LAG_PV, first, tail):
                    q, par = s - LAG_PV, ((u - LAG_PV) // BATCH_STEPS) % 2
                    pe.wait_ge(sem("pT_k1_done"), q + 1)
                    if (u - LAG_PV) % BATCH_STEPS == 0:
                        bq = (2 * B + (u - LAG_PV) // BATCH_STEPS)
                        pe.wait_ge(sem("v0_hi_done"), bq + 1)
                        pe.wait_ge(sem("v0_lo_done"), bq + 1)
                        pe.wait_ge(sem("v1_done"), bq + 1)
                    cols = [slice(KL, 3 * KL), slice(0, 2 * KL)]
                    c_ap = b_c[:, S:2 * S]
                    for h in range(2):
                        passes(c_ap, [(v0_hi[par][:, cols[h]], pT_hi[:, h]), (v0_lo[par][:, cols[h]], pT_hi[:, h])],
                               start=(h == 0), stop=False, chk=True)
                    for h in range(2):
                        passes(b_c[:, S + P:2 * S], [(v1[par][:, cols[h]], pT_k1[:, h])], start=False, stop=False,
                               chk=True)
                if live(u, LAG_WO, first, tail):
                    q, pq = s - LAG_WO, (u - LAG_WO) % BATCH_STEPS
                    pe.wait_ge(sem("ctx_lo_done"), q + 1)
                    if pq == 0:
                        if above_zero(2 * B + (u - LAG_WO) // BATCH_STEPS):
                            pe.wait_ge(sem("ln_r"), 2 * B + (u - LAG_WO) // BATCH_STEPS)
                    cp = (u - LAG_WO) % 2
                    for t in range(2):
                        tt = slice(t * P, (t + 1) * P)
                        mm = passes(b_o[:, t * D:(t + 1) * D],
                                    split3((ctx_hi[cp][:, tt], ctx_lo[cp][:, tt]),
                                           (wvo_hi[:, pq], wvo_lo[:, pq])),
                                    start=(pq == 0 and t == 0), stop=(pq == PAIRS - 1), chk=True)
                    mm.then_inc(sem("o_done"), 1)
                if live(u, LAG_PV, first, tail):
                    q = s - LAG_PV
                    pe.wait_ge(sem("pT_lo_done"), q + 1)
                    for h in range(2):
                        mm = passes(c_ap, [(v0_hi[par][:, cols[h]], pT_lo[:, h])], start=False, stop=(h == 1),
                                    chk=True)
                    mm.then_inc(sem("ctx_done"), 1)
                if p in (2, 4) and has_next(u, last, tail):
                    down(b + 1, p // 2 - 1)
                if p in (3, 5) and has_next(u, last, tail):
                    down_T(b + 1, p // 2 - 1)
                if p == 7 and has_prev(u, first):
                    n_down = 2 * (b + 2) if has_next(u, last, tail) else 2 * NB
                    pe.wait_ge(sem("cq_hi_done"), n_down)
                    pe.wait_ge(sem("cq_lo_done"), n_down)
                    pe.wait_ge(sem("kT_done"), n_down)
                    x1_T(b - 1, (u // BATCH_STEPS + 1) % 2)
                if live(u, LAG_QT, first, tail):
                    q, j = s - LAG_QT, (u % 2) * 2
                    qn = q_nat[((u - LAG_QT) // 2) % 2]
                    need = s if u % 2 == 0 else s - 1
                    pe.wait_ge(sem("qrope_done"), need)
                    if above_zero(q):
                        pe.wait_ge(sem("qT_lo_done"), q)
                    for t in range(2):
                        for h in range(2):
                            mm = pe.transpose(b_qT[:, (2 * t + h) * P:(2 * t + h + 1) * P], qn[t][:, j + h], ident[:])
                    mm.then_inc(sem("qTb_done"), 1)
                if live(u, LAG_SC, first, tail):
                    q, i, par = s - LAG_SC, (u - LAG_SC) % 2, ((u - LAG_SC) // BATCH_STEPS) % 2
                    pe.wait_ge(sem("qT_lo_done"), q + 1)
                    if (u - LAG_SC) % BATCH_STEPS == 0:
                        bq = 2 * B + (u - LAG_SC) // BATCH_STEPS
                        pe.wait_ge(sem("k_lo_done"), 2 * bq + 2)
                    if above_zero(4 * q):
                        pe.wait_ge(sem("masked_done"), 4 * q)
                    route_part(b, p, first)
                    for h in range(2):
                        pe.matmul(b_s[h][:, 0:P], qT[i][:, h], kT[par][:, 0:P], start=True, stop=True)
                        mm = passes(b_s[h][:, P:3 * P], split3((qT_hi[i][:, h], qT_lo[i][:, h]),
                                                               (k_hi[par][:], k_lo[par][:])))
                    mm.then_inc(sem("s_done"), 1)
                elif tail:
                    route_part(b, p, first)

            def route_part(b, p, first):
                if p == 0 and not first:
                    router(b - 2)
                if p == 3 and not first:
                    prefix(b - 2)

            pe.wait_ge(sem("tab_loaded"), 64)
            bodies(pe, step)

            def unit_T(n, par, last_y=None):
                pe.wait_ge(sem(f"xg{par}_loaded"), 32 * n + 64 - 32 * par)
                if last_y == "block":
                    pe.wait_ge(sem("y_copied"), 2 * (n - 2))
                if last_y == "shared, first":
                    pe.wait_ge(sem("y_added"), 2)
                if last_y == "shared":
                    pe.wait_ge(sem("y_added"), 2 * (n - 2 - NJ) + 2)
                for k in range(2):
                    for t in range(4):
                        mm = pe.transpose(b_y[k][:, t * P:(t + 1) * P], xg[par][:, t, k * P:(k + 1) * P], ident[:])
                    mm.then_inc(sem("unitT_done"), 1)

            def up(n, par, wpar, m):
                if above_zero(n):
                    pe.wait_ge(sem("h32_done"), 3 * (n - 1) + m + 1)
                w = MT[m]
                for bk, base in ((b_u[m], 0), (b_v[m], W3_AT)):
                    terms = []
                    for k in range(2):
                        a = base + k * HF + m * P
                        terms += split3((w13_hi[wpar][:, a:a + w], w13_lo[wpar][:, a:a + w]),
                                        (xh[par][:, k], xl[par][:, k]))
                    mm = passes(bk[0:w, :], terms)
                mm.then_inc(sem("up_done"), 1)

            def y_out(n, wpar):
                for j, ks in ((0, (0, 1)), (1, (0, 1)), (0, (2,)), (1, (2,))):
                    for k in ks:
                        pe.wait_ge(sem("h_lo_done"), 3 * n + k + 1)
                        w = MT[k]
                        for t in range(2):
                            tt = slice((2 * j + t) * P, (2 * j + t + 1) * P)
                            a = k * D
                            mm = passes(b_y[j][:, t * D:(t + 1) * D],
                                        split3((h_hi[0:w, k, tt], h_lo[0:w, k, tt]),
                                               (w2_hi[wpar][0:w, a:a + D], w2_lo[wpar][0:w, a:a + D])),
                                        start=(k == 0 and t == 0), stop=(k == 2), chk=True)
                    if ks == (2,):
                        mm.then_inc(sem("y_done"), 1)

            def split_ready(name, n):
                pe.wait_ge(sem(name + "_lo_done"), n + 1)

            def unit(n, par, wpar, last_wpar, weights=True, last_y=None, final=False):
                if weights:
                    split_ready("w13", n)
                pe.wait_ge(sem("xl_done"), 2 * n + 2)
                up(n, par, wpar, 0)
                if weights:
                    split_ready("w2", n - 1)
                y_out(n - 1, last_wpar)
                up(n, par, wpar, 1)
                if not final:
                    unit_T(n + 1, 1 - par, last_y)
                up(n, par, wpar, 2)

            router(NB - 1)
            unit_T(0, 0)
            pe.wait_ge(sem("xl_done"), 2)
            split_ready("w13", 0)
            up(0, 0, 0, 0)
            prefix(NB - 1)
            up(0, 0, 0, 1)
            pe.wait_ge(sem("prefix_read"), NB)
            up(0, 0, 0, 2)
            split_ready("w2", 0)
            y_out(0, 0)
            unit_T(1, 1, "shared, first")
            pe.wait_ge(sem("xl_done"), 4)
            split_ready("w13", 1)
            up(1, 1, 1, 0)
            up(1, 1, 1, 1)
            unit_T(2, 0)
            up(1, 1, 1, 2)
            unit(2, 0, 0, 1, last_y="block")
            with pe.Fori(1, NJ // 2) as i:
                unit(2 * i + 1, 1, 1, 0, last_y="block")
                unit(2 * i + 2, 0, 0, 1, last_y="block")
            unit(NJ, 1, 1, 0, last_y="block")
            unit(NJ + 1, 0, 0, 1, last_y="block")
            split_ready("w2", NJ + 1)
            with pe.Fori(NJ // 2 + 1, NU // 2 - 1) as i:
                unit(2 * i + 1, 1, 0, 0, False, "shared")
                unit(2 * i + 2, 0, 0, 0, False, "shared")
            unit(NU - 2, 1, 0, 0, False, "shared")
            unit(NU - 1, 0, 0, 0, False, final=True)
            y_out(NU - 1, 0)

        @block.scalar
        def _(act):
            act.dma_start(wk_nat[:], wkvb.rearrange("(h c) r -> c h r", h=H)[0:DN]).then_inc(sem("wkv_loaded"), 16)
            act.dma_start(wv_nat[:], wkvb.rearrange("(h c) r -> c h r", h=H)[DN:DN + DV]
                          ).then_inc(sem("wkv_loaded"), 16)
            with nc.allow_non_contiguous_dma(reason="norm weights, one value to a partition"):
                act.dma_start(aln_c[:, 0:1], aln[0:P].unsqueeze(1)).then_inc(sem("ln_w_loaded"), 16)
                act.dma_start(aln_c[0:HI, 1:2], aln[P:QL].unsqueeze(1)).then_inc(sem("ln_w_loaded"), 16)
                act.dma_start(aln_c[HI:P, 1:2], aln[P:QL].unsqueeze(1)).then_inc(sem("ln_w_loaded"), 16)
                act.dma_start(kvln2[0:KL], kvln.unsqueeze(1)).then_inc(sem("ln_w_loaded"), 16)
                act.dma_start(kvln2[KL:P], kvln.unsqueeze(1)).then_inc(sem("ln_w_loaded"), 16)
                act.dma_start(kvln1[0:KL], kvln.unsqueeze(1)).then_inc(sem("ln_w_loaded"), 16)

            def squares(b, t):
                idx = 2 * b + t
                act.wait_ge(sem("down_done"), idx + 1)
                if above_zero(idx - 1):
                    act.wait_ge(sem("rstd_done"), idx - 1)
                act.activation(sq[:, 0:QL], b_x[:, 0:QL], ACT.Square, scale=float(QL) ** -0.5,
                               accum_out=ss[:, t, 0:1]).then_inc(sem("ss_done"), 1)
                act.wait_ge(sem("ss_done"), 2 * idx + 1)
                act.activation(sq[:, 0:KL], b_x[:, QL:QL + KL], ACT.Square, scale=float(KL) ** -0.5,
                               accum_out=ss[:, t, 1:2]).then_inc(sem("ss_done"), 1)

            def normed(b, t):
                idx = 2 * b + t
                act.wait_ge(sem("rstd_done"), idx + 1)
                act.wait_ge(sem("kpe_done"), idx + 1)
                if above_zero(idx - 1):
                    act.wait_ge(sem("downT_done"), idx - 1)
                if above_zero(b):
                    act.wait_ge(sem("v0_hi_done"), b)
                    act.wait_ge(sem("v0_lo_done"), b)
                    act.wait_ge(sem("v1_done"), b)
                act.activation(an[:, t, 0:QL], b_x[:, 0:QL], ACT.Copy, scale=rstd[:, t, 0:1]
                               ).then_inc(sem("an_done"), 1)
                act.activation(an[:, t, QL:CKV], b_x[:, P:QL], ACT.Copy, scale=rstd[:, t, 0:1]
                               ).then_inc(sem("an_done"), 1)
                act.activation(an[:, t, CKV:CKV + KL], b_x[:, QL:QL + KL], ACT.Copy, scale=rstd[:, t, 1:2]
                               ).then_inc(sem("an_done"), 1)

            def down_hi(b, t, par):
                idx = 2 * b + t
                act.wait_ge(sem("downT_done"), idx + 1)
                if above_zero(BATCH_STEPS * (b - 1)):
                    act.wait_ge(sem("q_done"), BATCH_STEPS * (b - 1))
                    act.wait_ge(sem("s_done"), BATCH_STEPS * (b - 1))
                tt = slice(t * P, (t + 1) * P)
                act.activation(cq_hi[par][:, :, tt], b_x[:, 0:2 * P].rearrange("p (k n) -> p k n", k=2), ACT.Copy
                               ).then_inc(sem("cq_hi_done"), 1)
                act.activation(kT[par][:, tt], b_x[:, 2 * P:3 * P], ACT.Copy, scale=kvln1[:]
                               ).then_inc(sem("kT_done"), 1)

            act.wait_ge(sem("ln_w_loaded"), 96)
            act.wait_ge(sem("ones_done"), 1)
            def up_weights(i):
                k, g = divmod(i, 2)
                src = (b_q, b_qT, b_s[0], b_s[1])[i]
                act.wait_ge(sem("wm_done"), i + 1)
                act.activation(m_hi[:, k, 8 * g:8 * g + 8, 0:KL], src[:].rearrange("p (h c) -> p h c", h=8), ACT.Copy,
                               scale=aln_c[:, k:k + 1]).then_inc(sem("prep_hi"), 1)

            def value_weights(g):
                src = (b_pT, b_c, b_o, b_x)[g]
                act.wait_ge(sem("wvo_done"), g + 1)
                act.activation(wvo_hi[:, 2 * g:2 * g + 2], src[:].rearrange("p (i n) -> p i n", i=2), ACT.Copy,
                               scale=kvln2[:]).then_inc(sem("prep_hi"), 1)

            squares(0, 0)
            normed(0, 0)
            up_weights(0)
            up_weights(1)
            down_hi(0, 0, 0)
            up_weights(2)
            up_weights(3)
            act.wait_ge(sem("wpe_loaded"), 48)
            for k in range(2):
                act.activation(m_hi[:, k, :, KL:P], wq_pe[:, k], ACT.Copy, scale=aln_c[:, k:k + 1]
                               ).then_inc(sem("prep_hi"), 1)
            squares(0, 1)
            normed(0, 1)
            value_weights(0)
            value_weights(1)
            down_hi(0, 1, 0)
            value_weights(2)
            value_weights(3)

            def step(B, u, first, last, tail):
                s = BODY * B + u
                b, p = batch_of(B, u)
                if live(u, LAG_PV, first, tail):
                    q = s - LAG_PV
                    act.wait_ge(sem("pT_done"), q + 1)
                    if above_zero(q):
                        act.wait_ge(sem("ctx_done"), q)
                    act.activation(pT_hi[:], b_pT[:].rearrange("p (h n) -> p h n", h=2), ACT.Copy
                                   ).then_inc(sem("pT_hi_done"), 1)
                    act.activation(pT_k1[:], b_c[:, 0:2 * P].rearrange("p (h n) -> p h n", h=2), ACT.Copy
                                   ).then_inc(sem("pT_k1_done"), 1)
                if p in (3, 5) and has_next(u, last, tail):
                    normed(b + 1, p // 2 - 1)
                if live(u, LAG_SM, first, tail):
                    q, i = s - LAG_SM, (u - LAG_SM) % 2
                    if above_zero(q - 1):
                        act.wait_ge(sem("rden_done"), 2 * (q - 1))
                    for h in range(2):
                        for t in range(2):
                            z = 2 * h + t
                            act.wait_ge(sem("masked_done"), 4 * q + z + 1)
                            sc = probs[i][:, h, 0:P] if t == 0 else probs[i][:, h, P:3 * P]
                            act.activation(sc, sc, ACT.Exp, bias=negmax[i][:, z:z + 1], scale=-1.0,
                                           accum_out=psums[i][:, z:z + 1]).then_inc(sem("exp_done"), 1)
                if not tail:
                    t, qp = u % 2, (u // 2) % 2
                    act.wait_ge(sem("q_done"), s + 1)
                    if not (first and u < 4):
                        act.wait_ge(sem("qTb_done"), s - t - 2)
                    act.activation(q_nat[qp][t][:, :, 0:KL], b_q[:].rearrange("p (h c) -> p h c", h=4)[:, :, 0:KL],
                                   ACT.Copy).then_inc(sem("qlat_done"), 1)
                if live(u, LAG_PV, first, tail):
                    q, cp = s - LAG_PV, (u - LAG_PV) % 2
                    act.wait_ge(sem("ctx_done"), q + 1)
                    if above_zero(q - 1):
                        act.wait_ge(sem("o_done"), q - 1)
                    act.activation(ctx_hi[cp][:], b_c[:, S:2 * S], ACT.Copy).then_inc(sem("ctx_hi_done"), 1)
                if p in (2, 4) and has_next(u, last, tail):
                    squares(b + 1, p // 2 - 1)
                if p in (3, 5) and has_next(u, last, tail):
                    down_hi(b + 1, p // 2 - 1, (u // BATCH_STEPS + 1) % 2)
                if p == 7 and has_prev(u, first):
                    act.wait_ge(sem("x1T_done"), b)
                    if not first:
                        act.wait_ge(sem("logits_done"), b - 1)
                    act.activation(xt32[:], b_x[:].rearrange("p (k n) -> p k n", k=2), ACT.Copy
                                   ).then_inc(sem("x1t_read"), 1)
                if p == 5 and not first:
                    save_stash(b - 2, (u // BATCH_STEPS) % 2)
                if tail and p == 6:
                    w13_high(0, 0)
                    w2_high(0, 0)
                if not tail and p == 1:
                    fill(b)
                if live(u, LAG_QT, first, tail):
                    q, i = s - LAG_QT, (u - LAG_QT) % 2
                    act.wait_ge(sem("qTb_done"), q + 1)
                    if above_zero(q - 1):
                        act.wait_ge(sem("s_done"), q - 1)
                    act.activation(qT[i][:], b_qT[:, 0:S].rearrange("p (h n) -> p h n", h=2), ACT.Copy
                                   ).then_inc(sem("qT_done"), 1)
                    act.activation(qT_hi[i][:], b_qT[:, S:2 * S].rearrange("p (h n) -> p h n", h=2), ACT.Copy
                                   ).then_inc(sem("qT_hi_done"), 1)

            def fill(b):
                if above_zero(b):
                    act.wait_ge(sem("filled"), 16 * b)
                act.dma_start(x_sorted.rearrange("(e k p a) n -> k p e (a n)", e=E, k=NB, p=P)[b],
                              zeros[:].unsqueeze(1).to_broadcast([P, E, 2 * D])).then_inc(sem("filled"), 16)

            def save_stash(r, par):
                act.wait_ge(sem("route_step"), ROUTE_OPS * r + 17)
                act.activation(stash_all[:, bass.ds(r, 1)].rearrange("p a n -> p (a n)"), stash[par][:], ACT.Copy
                               ).then_inc(sem("stash_saved"), 1)

            def w13_high(n, par):
                act.wait_ge(sem("w13_loaded"), 16 * (n + 1))
                if above_zero(n - 1):
                    act.wait_ge(sem("up_done"), 3 * (n - 1))
                else:
                    act.wait_ge(sem("prep_lo"), 10)
                act.activation(w13_hi[par][:], w13_raw[:], ACT.Copy).then_inc(sem("w13_hi_done"), 1)

            def w2_high(n, par):
                act.wait_ge(sem("w2_loaded"), 16 * (n + 1))
                if above_zero(n - 1):
                    act.wait_ge(sem("y_done"), 2 * (n - 1))
                act.activation(w2_hi[par][:], w2_raw[:], ACT.Copy).then_inc(sem("w2_hi_done"), 1)

            act.wait_ge(sem("zeros_set"), 1)
            bodies(act, step)

            def x_round(n, par):
                for k in range(2):
                    act.wait_ge(sem("unitT_done"), 2 * n + k + 1)
                    act.activation(xh[par][:, k], b_y[k][:], ACT.Copy).then_inc(sem("xh_done"), 1)

            def gated(n, m):
                act.wait_ge(sem("up_done"), 3 * n + m + 1)
                if above_zero(n):
                    act.wait_ge(sem("h32_done"), 3 * (n - 1) + m + 1)
                w = MT[m]
                act.activation(silu[0:w, m], b_u[m][0:w, :], ACT.Silu).then_inc(sem("silu_done"), 1)

            def hidden_high(n, m):
                w = MT[m]
                act.wait_ge(sem("h32_done"), 3 * n + m + 1)
                if above_zero(n):
                    act.wait_ge(sem("y_done"), 2 * n)
                act.activation(h_hi[0:w, m], h32[0:w, m], ACT.Copy).then_inc(sem("h_hi_done"), 1)

            def copy_y(n, par, j):
                act.wait_ge(sem("y_done"), 2 * n + j + 1)
                if above_zero(n - 2 + par):
                    act.wait_ge(sem(f"y_stored{par}"), 8 * (n - 2 + par))
                act.activation(ys[par][:, 2 * j:2 * j + 2], b_y[j][:].rearrange("p (t n) -> p t n", t=2), ACT.Copy
                               ).then_inc(sem("y_copied"), 1)

            def finish(c, tiles=range(4)):
                for t in tiles:
                    act.wait_ge(sem("ln2_done"), c + 1)
                    a = acc[:, bass.ds(4 * c + t, 1)].rearrange("p a n -> p (a n)")
                    act.activation(a, a, ACT.Identity, bias=nb2[:, t:t + 1], scale=rs2[:, t:t + 1]
                                   ).then_inc(sem("out_ready"), 1)

            def unit(n, par, weights=True, last_block=True, final=False, done=None):
                gated(n, 0)
                if weights:
                    w13_high(n + 1, 1 - par)
                hidden_high(n, 0)
                if last_block:
                    copy_y(n - 1, 1 - par, 0)
                    copy_y(n - 1, 1 - par, 1)
                if done is not None:
                    finish(done, (0, 1))
                gated(n, 1)
                if not final:
                    x_round(n + 1, 1 - par)
                hidden_high(n, 1)
                if done is not None:
                    finish(done, (2, 3))
                gated(n, 2)
                hidden_high(n, 2)
                if weights:
                    w2_high(n + 1, 1 - par)

            x_round(0, 0)
            act.wait_ge(sem("ln_done"), 2 * NB)
            for m in range(3):
                gated(0, m)
            save_stash(NB - 1, 1)
            act.wait_ge(sem("stash_saved"), NB)
            act.activation(g_e[:], stash_all[:, :, 4:6], ACT.Exp).then_inc(sem("g_exp"), 1)
            for m in range(3):
                hidden_high(0, m)
            w13_high(1, 1)
            x_round(1, 1)
            w2_high(1, 1)
            unit(1, 1, last_block=False)
            unit(2, 0)
            unit(3, 1)
            with act.Fori(2, NJ // 2 + 1) as i:
                unit(2 * i, 0)
                unit(2 * i + 1, 1)
            unit(NJ + 1, 0, weights=False)
            unit(NJ + 2, 1, weights=False, last_block=False)
            unit(NJ + 3, 0, False, False, done=0)
            unit(NJ + 4, 1, False, False, done=1)
            unit(NJ + 5, 0, False, False, done=2)
            unit(NU - 2, 1, False, False, done=3)
            unit(NU - 1, 0, False, False, final=True, done=4)
            finish(NC - 3)
            finish(NC - 2)
            finish(NC - 1)

        @block.vector
        def _(dve):
            def lo(out_ap, full, hi, name):
                dve.tensor_tensor(out_ap, full, hi.bitcast(F32), ALU.subtract).then_inc(sem(name), 1)

            def x_low(b):
                dve.wait_ge(sem("xT_loaded"), 16 * (b + 1))
                dve.wait_ge(sem("xhi_done"), b + 1)
                if above_zero(2 * b):
                    dve.wait_ge(sem("down_done"), 2 * b)
                lo(x_lo[:], x_raw[:], x_hi[:], "xlo_done")

            def key_rope(b, t):
                idx = 2 * b + t
                dve.wait_ge(sem("ss_done"), 2 * idx + 2)
                if above_zero(idx - 1):
                    dve.wait_ge(sem("downT_done"), idx - 1)
                if above_zero(idx):
                    dve.wait_ge(sem("kpe_done"), idx)
                a = QL + KL
                hd = DR // 2
                dve.tensor_tensor(kr1[:], b_x[:, a:NA], cos[:, t], ALU.mult)
                dve.tensor_tensor(kr2[:, 0:hd], b_x[:, a + hd:NA], sgn[:, t, 0:hd], ALU.mult)
                dve.tensor_tensor(kr2[:, hd:DR], b_x[:, a:a + hd], sgn[:, t, hd:DR], ALU.mult
                                  ).then_inc(sem("kr_done"), 1)
                dve.wait_ge(sem("kr_done"), idx + 1)
                dve.tensor_tensor(an[:, t, CKV + KL:], kr1[:], kr2[:], ALU.add).then_inc(sem("kpe_done"), 1)

            def cq_low(b, t, par):
                idx = 2 * b + t
                dve.wait_ge(sem("cq_hi_done"), idx + 1)
                dve.wait_ge(sem("kT_done"), idx + 1)
                if above_zero(BATCH_STEPS * (b - 1)):
                    dve.wait_ge(sem("q_done"), BATCH_STEPS * (b - 1))
                tt = slice(t * P, (t + 1) * P)
                dve.tensor_tensor(cq_lo[par][:, tt], b_x[:, 0:P], cq_hi[par][:, 0, tt].bitcast(F32), ALU.subtract)
                under = cq_hi[par][HI:P, 1, tt]
                lo(under, b_x[HI:P, P:2 * P], under, "cq_lo_done")

            def k_low(b, t, par):
                tt = slice(t * P, (t + 1) * P)
                dve.wait_ge(sem("k_hi_done"), 2 * b + t + 1)
                if above_zero(BATCH_STEPS * (b - 1)):
                    dve.wait_ge(sem("s_done"), BATCH_STEPS * (b - 1))
                lo(k_lo[par][:, tt], kT[par][:, tt], k_hi[par][:, tt], "k_lo_done")

            def v_low(b, par):
                dve.wait_ge(sem("v0_hi_done"), b + 1)
                if above_zero(BATCH_STEPS * (b - 1)):
                    dve.wait_ge(sem("ctx_done"), BATCH_STEPS * (b - 1))
                dve.wait_ge(sem("pads_done"), 1)
                lo(v0_lo[par][:, KL:2 * KL], an[:, 0, CKV:CKV + KL], v0_hi[par][:, KL:2 * KL], "v0_lo_done")

            dve.memset(zeros[:], 0.0).then_inc(sem("zeros_set"), 1)
            dve.memset(kvln1[KL:P], 1.0).then_inc(sem("ones_done"), 1)
            dve.wait_ge(sem("wa_loaded"), 16)
            dve.wait_ge(sem("wa_hi_done"), 1)
            lo(wa_lo[:], wa_raw[:], wa_hi[:], "wa_lo_done")
            x_low(0)
            dve.wait_ge(sem("rope_loaded"), 64)
            def prep_low(i, dst, src, scale, hi):
                dve.wait_ge(sem("prep_hi"), i)
                dve.scalar_tensor_tensor(out=dst, in0=src, scalar=scale, in1=hi.bitcast(F32), op0=ALU.mult,
                                         op1=ALU.subtract).then_inc(sem("prep_lo"), 1)

            def value_low(g):
                prep_low(7 + g, wvo_lo[:, 2 * g:2 * g + 2], (b_pT, b_c, b_o, b_x)[g][:].rearrange(
                    "p (i n) -> p i n", i=2), kvln2[:], wvo_hi[:, 2 * g:2 * g + 2])

            key_rope(0, 0)
            dve.wait_ge(sem("ln_w_loaded"), 96)
            for k, rows in ((0, P), (1, HI)):
                if k == 1:
                    cq_low(0, 0, 0)
                    k_low(0, 0, 0)
                for g in range(2):
                    i = 2 * k + g
                    prep_low(i + 1, m_lo[0:rows, k, 8 * g:8 * g + 8, 0:KL],
                             (b_q, b_qT, b_s[0], b_s[1])[i][0:rows, :].rearrange("p (h c) -> p h c", h=8),
                             aln_c[0:rows, k:k + 1], m_hi[0:rows, k, 8 * g:8 * g + 8, 0:KL])
            dve.wait_ge(sem("wpe_loaded"), 48)
            for k, rows in ((0, P), (1, HI)):
                prep_low(5 + k, m_lo[0:rows, k, :, KL:P], wq_pe[0:rows, k], aln_c[0:rows, k:k + 1],
                         m_hi[0:rows, k, :, KL:P])
            key_rope(0, 1)
            value_low(0)
            value_low(1)
            cq_low(0, 1, 0)
            k_low(0, 1, 0)
            v_low(0, 0)
            value_low(2)
            value_low(3)
            dve.wait_ge(sem("mask_done"), 1)

            def step(B, u, first, last, tail):
                s = BODY * B + u
                b, p = batch_of(B, u)
                npar = (u // BATCH_STEPS + 1) % 2
                xpar = 1 - (u // BATCH_STEPS) % 2

                def between(slot):
                    if p in SLOTS and not first and SLOTS[p][0] + slot < SLOTS[p][1]:
                        route_op(b - 2, SLOTS[p][0] + slot, 1 - xpar)

                if live(u, LAG_PV, first, tail):
                    q = s - LAG_PV
                    dve.wait_ge(sem("pT_hi_done"), q + 1)
                    if above_zero(q):
                        dve.wait_ge(sem("ctx_done"), q)
                    lo(pT_lo[:], b_pT[:].rearrange("p (h n) -> p h n", h=2), pT_hi[:], "pT_lo_done")
                between(0)
                if live(u, LAG_SM, first, tail):
                    q, i = s - LAG_SM, (u - LAG_SM) % 2
                    if above_zero(4 * (q - 1)):
                        dve.wait_ge(sem("norm_done"), 4 * (q - 1))
                    for h in range(2):
                        dve.wait_ge(sem("exp_done"), 4 * q + 2 * h + 2)
                        dve.reciprocal(rden[i][:, 2 * h:2 * h + 2], psums[i][:, 2 * h:2 * h + 2]
                                       ).then_inc(sem("rden_done"), 1)
                between(1)
                if not tail:
                    t = u % 2
                    dve.wait_ge(sem("qlat_done"), s + 1)
                    if above_zero(s):
                        dve.wait_ge(sem("qrope_done"), s)
                    hd = DR // 2
                    bq = b_q[:].rearrange("p (h c) -> p h c", h=4)
                    dve.tensor_tensor(r1[:], bq[:, :, KL:P], cos[:, t].unsqueeze(1).to_broadcast([P, 4, DR]), ALU.mult)
                    dve.tensor_tensor(r2[:, :, 0:hd], bq[:, :, KL + hd:P],
                                      sgn[:, t, 0:hd].unsqueeze(1).to_broadcast([P, 4, hd]), ALU.mult)
                    dve.tensor_tensor(r2[:, :, hd:DR], bq[:, :, KL:KL + hd],
                                      sgn[:, t, hd:DR].unsqueeze(1).to_broadcast([P, 4, hd]), ALU.mult
                                      ).then_inc(sem("rope_done"), 1)
                between(2)
                if live(u, LAG_PV, first, tail):
                    q, cp = s - LAG_PV, (u - LAG_PV) % 2
                    dve.wait_ge(sem("ctx_hi_done"), q + 1)
                    if above_zero(q - 1):
                        dve.wait_ge(sem("o_done"), q - 1)
                    lo(ctx_lo[cp][:], b_c[:, S:2 * S], ctx_hi[cp][:], "ctx_lo_done")
                between(3)
                if p == 6 and has_prev(u, first):
                    dve.wait_ge(sem("lnr_done"), b)
                    for t in range(2):
                        dve.tensor_scalar(xs[xpar][:, t], xs[xpar][:, t], mv[:, t, 0:1], lnr[:, t:t + 1], ALU.subtract,
                                          ALU.mult).then_inc(sem("ln_done"), 1)
                if has_next(u, last, tail):
                    if p in (4, 6):
                        k_low(b + 1, p // 2 - 2, npar)
                    if p == 7:
                        v_low(b + 1, npar)
                between(4)
                if p == 1 and has_next(u, last, tail):
                    x_low(b + 1)
                if p in (2, 4) and has_next(u, last, tail):
                    key_rope(b + 1, p // 2 - 1)
                if p in (3, 5) and has_next(u, last, tail):
                    cq_low(b + 1, p // 2 - 1, npar)
                if p == 5 and has_prev(u, first):
                    dve.wait_ge(sem("o_done"), BATCH_STEPS * b)
                    dve.wait_ge(sem("xnat_loaded"), 16 * b)
                    if above_zero(b - 1):
                        dve.wait_ge(sem("x1T_done"), b - 1)
                    if above_zero(b - 2):
                        dve.wait_ge(sem("scattered"), 64 * (b - 2))
                    if above_zero(b - 1 - xpar):
                        dve.wait_ge(sem(f"x1_stored{xpar}"), 8 * (b - 1 - xpar))
                    if above_zero(2 * (b - 1)):
                        dve.wait_ge(sem("ln_done"), 2 * (b - 1))
                    dve.tensor_tensor(xs[xpar][:], b_o[:].rearrange("p (t n) -> p t n", t=2), x_nat[:], ALU.add
                                      ).then_inc(sem("ln_r"), 1)
                if tail and p == 7:
                    w13_low(0, 0)
                    w2_low(0, 0)
                if live(u, LAG_QT, first, tail):
                    q, i = s - LAG_QT, (u - LAG_QT) % 2
                    dve.wait_ge(sem("qT_hi_done"), q + 1)
                    if above_zero(q - 1):
                        dve.wait_ge(sem("s_done"), q - 1)
                    lo(qT_lo[i][:], b_qT[:, S:2 * S].rearrange("p (h n) -> p h n", h=2), qT_hi[i][:], "qT_lo_done")
                between(5)
                if live(u, LAG_SC, first, tail):
                    q, i = s - LAG_SC, (u - LAG_SC) % 2
                    dve.wait_ge(sem("s_done"), q + 1)
                    if above_zero(q - 1):
                        dve.wait_ge(sem("pT_done"), q - 1)
                    if above_zero(4 * (q - 1)):
                        dve.wait_ge(sem("exp_done"), 4 * (q - 1))
                    if above_zero(4 * q):
                        dve.wait_ge(sem("masked_done"), 4 * q)
                    hold_dve(10)
                    route_read(b, p, first)
                    for h in range(2):
                        for t in range(2):
                            cols = slice(0, P) if t == 0 else slice(P, 3 * P)
                            mk = mask[:, P:S] if t == 0 else mask[:]
                            dve.tensor_tensor_reduce(out=probs[i][:, h, cols], in0=b_s[h][:, cols], in1=mk,
                                                     scale=-SCALE, scalar=3e38, op0=ALU.add, op1=ALU.min,
                                                     accum_out=negmax[i][:, 2 * h + t:2 * h + t + 1]
                                                     ).then_inc(sem("masked_done"), 1)
                elif tail:
                    route_read(b, p, first)
                between(6)
                if p == 5 and has_prev(u, first):
                    dve.wait_ge(sem("ln_r"), b)
                    if above_zero(2 * (b - 1)):
                        dve.wait_ge(sem("bst_done"), 2 * (b - 1))
                    hold_dve(8)
                    for t in range(2):
                        dve.bn_stats(bst[:, t], xs[xpar][:, t]).then_inc(sem("bst_done"), 1)
                    for t in range(2):
                        dve.wait_ge(sem("bst_done"), 2 * b - 1 + t)
                        if above_zero(2 * (b - 1) + t):
                            dve.wait_ge(sem("mv_done"), 2 * (b - 1) + t)
                        hold_dve(9)
                        dve.bn_aggr(mv[:, t], bst[:, t]).then_inc(sem("mv_done"), 1)

            def route_read(b, p, first):
                if p == 0 and not first:
                    read_logits(b - 2)
                if p == 3 and not first:
                    read_prefix(b - 2)

            def read_logits(r):
                dve.wait_ge(sem("logits_done"), r + 1)
                dve.tensor_copy(lg[:], b_s[0][:, 3 * P:3 * P + 2 * E].rearrange("p (t e) -> p t e", t=2)
                                ).then_inc(sem("lg_read"), 1)

            def read_prefix(r):
                dve.wait_ge(sem("prefix_done"), r + 1)
                dve.tensor_copy(pfx[:], b_s[0][:, 3 * P:3 * P + 3 * E].rearrange("p (t e) -> p t e", t=3)
                                ).then_inc(sem("prefix_read"), 1)

            def route_op(r, i, par):
                if i == 0:
                    dve.wait_ge(sem("lg_read"), r + 1)
                else:
                    dve.wait_ge(sem("route_step"), ROUTE_OPS * r + i)
                if i == 13:
                    dve.wait_ge(sem("prefix_read"), r + 1)
                if i in (12, 16) and above_zero(r - 1):
                    dve.wait_ge(sem("stash_saved"), r - 1)
                if i == 17 and above_zero(r - 1):
                    dve.wait_ge(sem("scattered"), 64 * (r - 1))
                c = 0 if i < 5 else 1
                src = lg if c == 0 else lg2
                over = lambda a: a.unsqueeze(2).to_broadcast([P, 2, E])
                if i in (0, 6):
                    ins = dve.tensor_reduce(r_m[:, c], src[:], AX.X, ALU.max)
                elif i in (1, 7):
                    ins = dve.tensor_tensor(r_eq[:], src[:], over(r_m[:, c]), ALU.is_equal)
                elif i in (2, 8):
                    ranks = tab[:, T_RANK:T_RANK + E].unsqueeze(1).to_broadcast([P, 2, E])
                    ins = dve.tensor_tensor(r_w[:], r_eq[:], ranks, ALU.mult)
                elif i in (3, 9):
                    ins = dve.tensor_reduce(r_r[:, c], r_w[:], AX.X, ALU.max)
                elif i in (4, 10):
                    ins = dve.tensor_tensor(sel[:, c], r_w[:], over(r_r[:, c]), ALU.is_equal)
                elif i == 5:
                    ins = dve.scalar_tensor_tensor(out=lg2[:], in0=sel[:, 0], scalar=-3e38, in1=lg[:],
                                                   op0=ALU.mult, op1=ALU.add)
                elif i == 11:
                    ins = dve.tensor_tensor(picked[:], sel[:, 0], sel[:, 1], ALU.add)
                elif i == 12:
                    ins = dve.tensor_tensor(stash[par][:, 4:6], r_m[:, 1], r_m[:, 0], ALU.subtract)
                elif i == 13:
                    ins = dve.tensor_tensor(posf[:], pfx[:, 0:2], run[par][:].unsqueeze(1).to_broadcast([P, 2, E]),
                                            ALU.add)
                elif i == 14:
                    ins = dve.tensor_tensor(run[1 - par][:], run[par][:], pfx[:, 2], ALU.add)
                elif i == 15:
                    ins = dve.tensor_tensor(posw[:], sel[:], posf[:].unsqueeze(1).to_broadcast([P, 2, 2, E]), ALU.mult)
                elif i == 16:
                    ins = dve.tensor_reduce(stash[par][:, 0:4].rearrange("p (k t) -> p k t", k=2), posw[:], AX.X,
                                            ALU.add)
                else:
                    ins = dve.tensor_copy(pos_i[par][:], stash[par][:, 0:4])
                ins.then_inc(sem("route_step"), 1)

            def w13_low(n, par):
                dve.wait_ge(sem("w13_hi_done"), n + 1)
                if above_zero(n - 1):
                    dve.wait_ge(sem("up_done"), 3 * (n - 1))
                lo(w13_lo[par][:], w13_raw[:], w13_hi[par][:], "w13_lo_done")

            def w2_low(n, par):
                dve.wait_ge(sem("w2_hi_done"), n + 1)
                if above_zero(n - 1):
                    dve.wait_ge(sem("y_done"), 2 * (n - 1))
                lo(w2_lo[par][:], w2_raw[:], w2_hi[par][:], "w2_lo_done")

            dve.wait_ge(sem("tab_loaded"), 64)
            dve.tensor_copy(tri_b[:], tri[:])
            dve.tensor_copy(ones_b[:], ones[:])
            dve.tensor_copy(run[0][:], tab[:, T_REGION:T_REGION + E]).then_inc(sem("run_set"), 1)
            dve.wait_ge(sem("run_set"), 1)
            bodies(dve, step)

            steps = [0]

            def g(ins):
                steps[0] += 1
                ins.then_inc(sem("table_step"), 1)
                dve.wait_ge(sem("table_step"), steps[0])

            def block_tables():
                def col(a, n=E):
                    return tab[:, a:a + n]
                je = [P, NJ, E]
                last = run[0][:]
                g(dve.tensor_tensor(t_n[:], last, col(T_REGION), ALU.subtract))
                g(dve.tensor_tensor(t_cmp[:], t_n[:].unsqueeze(2).to_broadcast([P, E, E]),
                                    col(T_THR).unsqueeze(1).to_broadcast([P, E, E]), ALU.is_gt))
                g(dve.tensor_reduce(t_nb[:], t_cmp[:], AX.X, ALU.add))
                g(dve.tensor_tensor(t_cum[:], t_nb[:].unsqueeze(1).to_broadcast([P, E, E]),
                                    col(T_LTRI, E * E).rearrange("p (a b) -> p a b", a=E), ALU.mult))
                g(dve.tensor_reduce(t_end[:], t_cum[:], AX.X, ALU.add))
                g(dve.tensor_tensor(t_start[:], t_end[:], t_nb[:], ALU.subtract))
                g(dve.tensor_scalar(t_j[:], col(T_J1, NJ), t_end[:, E - 1:E], 1.0, ALU.min, ALU.subtract))
                g(dve.tensor_tensor(t_ge[:], t_j[:].unsqueeze(2).to_broadcast(je),
                                    t_start[:].unsqueeze(1).to_broadcast(je), ALU.is_ge))
                g(dve.tensor_tensor(t_lt[:], t_end[:].unsqueeze(1).to_broadcast(je),
                                    t_j[:].unsqueeze(2).to_broadcast(je), ALU.is_gt))
                g(dve.tensor_tensor(t_oh[:], t_ge[:], t_lt[:], ALU.mult))
                for i, a in enumerate((col(T_EIDX), t_n[:], t_start[:])):
                    ins = dve.tensor_tensor(t_w[:, i], t_oh[:], a.unsqueeze(1).to_broadcast(je), ALU.mult)
                g(ins)
                g(dve.tensor_reduce(t_sum[:], t_w[:], AX.X, ALU.add))
                g(dve.tensor_scalar(t_wrow[:], t_sum[:, 0], float(P), tab[:, T_P:T_P + 1], ALU.mult, ALU.add))
                dve.tensor_copy(wrow_i[:], t_wrow[:]).then_inc(sem("wrows_ready"), 1)
                g(dve.tensor_tensor(t_k0[:], t_j[:], t_sum[:, 2], ALU.subtract))
                g(dve.tensor_scalar(t_k1[:], t_k0[:], float(C), 0.0, ALU.mult, ALU.add))
                g(dve.tensor_tensor(t_k[:], t_k1[:].unsqueeze(2).to_broadcast([P, NJ, 4]),
                                    col(T_TP, 4).unsqueeze(1).to_broadcast([P, NJ, 4]), ALU.add))
                g(dve.tensor_scalar(t_last[:], t_sum[:, 1], 1.0, -1.0, ALU.mult, ALU.add))
                g(dve.tensor_tensor(t_km[:], t_k[:], t_last[:].unsqueeze(2).to_broadcast([P, NJ, 4]), ALU.min))
                g(dve.tensor_scalar(t_base[:], t_sum[:, 0], float(REGION), 0.0, ALU.mult, ALU.add))
                g(dve.tensor_tensor(t_row[:], t_km[:], t_base[:].unsqueeze(2).to_broadcast([P, NJ, 4]), ALU.add))
                dve.tensor_copy(row_i[:], t_row[:]).then_inc(sem("rows_ready"), 1)

            def result_tables():
                shape = [P, NB, 4, E]
                g(dve.tensor_scalar(t_s512[:], t_start[:], float(C), 0.0, ALU.mult, ALU.add))
                dve.memset(t_delta[:, 0:1], 0.0)
                g(dve.tensor_tensor(t_delta[:, 1:E + 1], t_s512[:], tab[:, T_REGION:T_REGION + E], ALU.subtract))
                g(dve.tensor_tensor(t_dd[:], t_delta[:, 1:E + 1], t_delta[:, 0:E], ALU.subtract))
                dve.wait_ge(sem("stash_saved"), NB)
                rows = stash_all[:, :, 0:4]
                g(dve.tensor_tensor(t_in[:], rows.unsqueeze(3).to_broadcast(shape),
                                    tab[:, T_REGION:T_REGION + E].unsqueeze(1).unsqueeze(1).to_broadcast(shape),
                                    ALU.is_ge))
                g(dve.tensor_tensor(t_inw[:], t_in[:], t_dd[:].unsqueeze(1).unsqueeze(1).to_broadcast(shape),
                                    ALU.mult))
                g(dve.tensor_reduce(t_shift[:], t_inw[:], AX.X, ALU.add))
                g(dve.tensor_tensor(t_y[:], rows, t_shift[:], ALU.add))
                dve.tensor_copy(yrow_i[:], t_y[:]).then_inc(sem("yrows_ready"), 1)
                dve.wait_ge(sem("g_exp"), 1)
                g(dve.tensor_scalar(g_den[:], g_e[:], 1.0, None, ALU.add))
                g(dve.reciprocal(g_1[:].rearrange("p (b t) -> p b t", b=NB), g_den[:]))
                g(dve.tensor_tensor(g_2[:].rearrange("p (b t) -> p b t", b=NB), g_e[:],
                                    g_1[:].rearrange("p (b t) -> p b t", b=NB), ALU.mult))

            def unit_low(n, par):
                for k in range(2):
                    dve.wait_ge(sem("xh_done"), 2 * n + k + 1)
                    lo(xl[par][:, k], b_y[k][:], xh[par][:, k], "xl_done")

            def hidden(n, m):
                w = MT[m]
                dve.wait_ge(sem("silu_done"), 3 * n + m + 1)
                if above_zero(n):
                    dve.wait_ge(sem("h_hi_done"), 3 * (n - 1) + m + 1)
                    dve.wait_ge(sem("h_lo_done"), 3 * (n - 1) + m + 1)
                dve.tensor_tensor(h32[0:w, m], b_v[m][0:w, :], silu[0:w, m], ALU.mult).then_inc(sem("h32_done"), 1)

            def hidden_low(n, m):
                w = MT[m]
                dve.wait_ge(sem("h_hi_done"), 3 * n + m + 1)
                dve.wait_ge(sem("h32_done"), 3 * n + m + 1)
                lo(h_lo[0:w, m], h32[0:w, m], h_hi[0:w, m], "h_lo_done")

            def add_shared(n, c):
                for j in range(2):
                    dve.wait_ge(sem("y_done"), 2 * n + j + 1)
                    a = acc[:, bass.ds(4 * c + 2 * j, 2)]
                    dve.tensor_tensor(a, b_y[j][:].rearrange("p (t n) -> p t n", t=2), a, ALU.add
                                      ).then_inc(sem("y_added"), 1)

            def combine(c, par, choices=(0, 1)):
                dve.wait_ge(sem(f"yg{par}_loaded"), 64 * c + 128 - 64 * par)
                dve.wait_ge(sem("y_added"), 2 * c + 2)
                for k in choices:
                    gate = (g_1, g_2)[k]
                    for t in range(4):
                        if k == 1:
                            dve.wait_ge(sem("combine_step"), 8 * c + t + 1)
                        a = acc[:, bass.ds(4 * c + t, 1)].rearrange("p a n -> p (a n)")
                        dve.scalar_tensor_tensor(out=a, in0=yg[par][:, k, t], scalar=gate[:, bass.ds(4 * c + t, 1)],
                                                 in1=a, op0=ALU.mult, op1=ALU.add).then_inc(sem("combine_step"), 1)

            def norm_stats(c):
                dve.wait_ge(sem("combine_step"), 8 * c + 8)
                if above_zero(c):
                    dve.wait_ge(sem("out_ready"), 4 * c)
                    dve.wait_ge(sem("bst2_done"), 4 * c)
                hold_dve(11)
                for t in range(4):
                    a = acc[:, bass.ds(4 * c + t, 1)].rearrange("p a n -> p (a n)")
                    dve.bn_stats(bst2[:, t], a).then_inc(sem("bst2_done"), 1)
                for t in range(4):
                    dve.wait_ge(sem("bst2_done"), 4 * c + t + 1)
                    if above_zero(4 * c + t):
                        dve.wait_ge(sem("mv2_done"), 4 * c + t)
                    hold_dve(12)
                    dve.bn_aggr(mv2[:, t], bst2[:, t]).then_inc(sem("mv2_done"), 1)

            def unit(n, par, weights=True, added=None, combined=None, final=False):
                hidden(n, 0)
                if added is not None:
                    add_shared(n - 1, added)
                hidden_low(n, 0)
                if weights:
                    w13_low(n + 1, 1 - par)
                hidden(n, 1)
                if not final:
                    unit_low(n + 1, 1 - par)
                if combined is not None:
                    combine(combined, 1 - par, (0,))
                hidden_low(n, 1)
                if combined is not None:
                    combine(combined, 1 - par, (1,))
                hidden(n, 2)
                hidden_low(n, 2)
                if combined is not None:
                    norm_stats(combined)
                if weights:
                    w2_low(n + 1, 1 - par)

            read_logits(NB - 1)
            unit_low(0, 0)
            for i in range(13):
                route_op(NB - 1, i, 1)
            read_prefix(NB - 1)
            for i in range(13, ROUTE_OPS):
                route_op(NB - 1, i, 1)
            dve.wait_ge(sem("route_step"), ROUTE_OPS * NB)
            block_tables()
            for m in range(3):
                hidden(0, m)
                hidden_low(0, m)
            w13_low(1, 1)
            dve.wait_ge(sem("acc_loaded"), 16)
            add_shared(0, 0)
            unit_low(1, 1)
            w2_low(1, 1)
            unit(1, 1)
            result_tables()
            with dve.Fori(1, NJ // 2 + 1) as i:
                unit(2 * i, 0)
                unit(2 * i + 1, 1)
            unit(NJ + 1, 0, weights=False)
            unit(NJ + 2, 1, False, 1, 0)
            with dve.Fori(1, NC // 2 - 1) as i:
                unit(NJ + 1 + 2 * i, 0, False, 2 * i, 2 * i - 1)
                unit(NJ + 2 + 2 * i, 1, False, 2 * i + 1, 2 * i)
            unit(NU - 1, 0, False, NC - 2, NC - 3, final=True)
            combine(NC - 2, 0)
            norm_stats(NC - 2)
            add_shared(NU - 1, NC - 1)
            combine(NC - 1, 1)
            norm_stats(NC - 1)

        @block.gpsimd
        def _(pool):
            def hi(out_ap, in_ap, name):
                pool.tensor_scalar(out_ap, in_ap, 1.0, 0.0, ALU.mult, ALU.add).then_inc(sem(name), 1)

            def x_high(b):
                pool.wait_ge(sem("xT_loaded"), 16 * (b + 1))
                if above_zero(2 * b):
                    pool.wait_ge(sem("down_done"), 2 * b)
                if above_zero(b):
                    pool.wait_ge(sem("xhi_done"), b)
                hold_pool(0)
                hi(x_hi[:], x_raw[:], "xhi_done")

            def inv_rms(b, t):
                idx = 2 * b + t
                pool.wait_ge(sem("ss_done"), 2 * idx + 2)
                if above_zero(2 * (idx - 1)):
                    pool.wait_ge(sem("an_done"), 3 * (idx - 1))
                if above_zero(idx):
                    pool.wait_ge(sem("ms_done"), idx)
                hold_pool(1)
                pool.tensor_scalar(ms[:, t], ss[:, t], 1.0, RMS_EPS, ALU.mult, ALU.add).then_inc(sem("ms_done"), 1)
                pool.wait_ge(sem("ms_done"), idx + 1)
                pool.tensor_tensor(rstd[:, t], ms[:, t], mhalf[:], ALU.pow).then_inc(sem("rstd_done"), 1)

            def k_high(b, t, par):
                tt = slice(t * P, (t + 1) * P)
                pool.wait_ge(sem("kT_done"), 2 * b + t + 1)
                if above_zero(BATCH_STEPS * (b - 1)):
                    pool.wait_ge(sem("s_done"), BATCH_STEPS * (b - 1))
                if above_zero(2 * b + t):
                    pool.wait_ge(sem("k_hi_done"), 2 * b + t)
                hold_pool(2)
                hi(k_hi[par][:, tt], kT[par][:, tt], "k_hi_done")

            def values(b, par):
                pool.wait_ge(sem("an_done"), 3 * (2 * b + 2))
                if above_zero(BATCH_STEPS * (b - 1)):
                    pool.wait_ge(sem("ctx_done"), BATCH_STEPS * (b - 1))
                if above_zero(b):
                    pool.wait_ge(sem("v1_done"), b)
                hold_pool(3)
                hi(v0_hi[par][:, KL:2 * KL], an[:, 0, CKV:CKV + KL], "v0_hi_done")
                hi(v1[par][:, KL:2 * KL], an[:, 1, CKV:CKV + KL], "v1_done")

            pool.memset(held_in[:], 0.0).then_inc(sem("held_set"), 1)
            pool.wait_ge(sem("held_set"), 1)
            pool.wait_ge(sem("wa_loaded"), 16)
            hi(wa_hi[:], wa_raw[:], "wa_hi_done")
            x_high(0)
            pool.memset(mhalf[:], -0.5).then_inc(sem("mhalf_set"), 1)
            pool.wait_ge(sem("mhalf_set"), 1)
            pool.memset(ident[:], 0.0).then_inc(sem("pool_set"), 1)
            pool.memset(mask[:], 0.0).then_inc(sem("pool_set"), 1)
            for i in range(2):
                for j in (slice(0, KL), slice(2 * KL, 3 * KL)):
                    pool.memset(v0_hi[i][:, j].bitcast(F32), 0.0)
                    pool.memset(v0_lo[i][:, j].bitcast(F32), 0.0)
                    ins = pool.memset(v1[i][:, j], 0.0)
            ins.then_inc(sem("pads_done"), 1)
            pool.wait_ge(sem("pool_set"), 2)
            pool.affine_select(out=ident[:], in_=ident[:], compare_op=ALU.not_equal, fill=1.0, base=0,
                               pattern=[[-1, P]], channel_multiplier=1).then_inc(sem("ident_done"), 1)
            pool.affine_select(out=mask[:, P:S], in_=mask[:, P:S], compare_op=ALU.is_ge, fill=MASKED, base=0,
                               pattern=[[-1, P]], channel_multiplier=1).then_inc(sem("mask_done"), 1)
            pool.wait_ge(sem("pads_done"), 1)
            for t in range(2):
                inv_rms(0, t)
                k_high(0, t, 0)
            values(0, 0)
            pool.dma_start(w13_raw[:], w13_all[0:P]).then_inc(sem("w13_loaded"), 16)
            pool.dma_start(w2_raw[:], w2_all[0:P]).then_inc(sem("w2_loaded"), 16)

            def step(B, u, first, last, tail):
                s = BODY * B + u
                b, p = batch_of(B, u)
                nx = has_next(u, last, tail)
                npar = (u // BATCH_STEPS + 1) % 2
                if live(u, LAG_SM, first, tail):
                    q, i = s - LAG_SM, (u - LAG_SM) % 2
                    for h in range(2):
                        pool.wait_ge(sem("rden_done"), 2 * q + h + 1)
                        if above_zero(4 * q + 2 * h):
                            pool.wait_ge(sem("norm_done"), 4 * q + 2 * h)
                        hold_pool(4)
                        for t in range(2):
                            cols = slice(0, P) if t == 0 else slice(P, 3 * P)
                            z = 2 * h + t
                            pool.tensor_scalar(probs[i][:, h, cols], probs[i][:, h, cols], rden[i][:, z:z + 1], 1.0,
                                               ALU.mult, ALU.mult).then_inc(sem("norm_done"), 1)
                if not tail:
                    t, qp = u % 2, (u // 2) % 2
                    pool.wait_ge(sem("rope_done"), s + 1)
                    if not (first and u < 4):
                        pool.wait_ge(sem("qTb_done"), s - t - 2)
                    pool.tensor_tensor(q_nat[qp][t][:, :, KL:P], r1[:], r2[:], ALU.add).then_inc(sem("qrope_done"), 1)
                if p == 0 and nx:
                    x_high(b + 1)
                if p in (2, 4) and nx:
                    inv_rms(b + 1, p // 2 - 1)
                if p in (3, 5) and nx:
                    k_high(b + 1, p // 2 - 1, npar)
                if p == 6 and nx:
                    values(b + 1, npar)
                if tail and p == 0:
                    pool.wait_ge(sem("prep_lo"), 10)
                    pool.wait_ge(sem("x1_stored0"), 16 * (NB // 2 - 1))
                    pool.wait_ge(sem("x1_stored1"), 16 * (NB // 2 - 1))
                    pool.dma_start(xg[0][:], x1_v[:, 0:4]).then_inc(sem("xg0_loaded"), 64)
                if p in (6, 7) and not first:
                    scatter(b - 2, (u // BATCH_STEPS) % 2, p - 6)
                if p == 5 and has_prev(u, first):
                    pool.wait_ge(sem("mv_done"), 2 * b)
                    if above_zero(2 * (b - 1)):
                        pool.wait_ge(sem("ln_done"), 2 * (b - 1))
                    if above_zero(b - 1):
                        pool.wait_ge(sem("vps_done"), b - 1)
                    hold_pool(5)
                    pool.tensor_scalar(vps[:], mv[:, :, 1], 1.0, LN_EPS, ALU.mult, ALU.add
                                       ).then_inc(sem("vps_done"), 1)
                    pool.wait_ge(sem("vps_done"), b)
                    pool.tensor_tensor(lnr[:], vps[:], mhalf[:], ALU.pow).then_inc(sem("lnr_done"), 1)

            x1_v = x1_dram.rearrange("b (t p) n -> p (b t) n", p=P)

            def scatter(r, par, k):
                pool.wait_ge(sem("route_step"), ROUTE_OPS * r + ROUTE_OPS)
                pool.wait_ge(sem("filled"), 16 * (r + 1))
                if above_zero(32 * (2 * r + k)):
                    pool.wait_ge(sem("scattered"), 32 * (2 * r + k))
                if above_zero(2 * r + k):
                    pool.wait_ge(sem("scatter_held"), 2 * r + k)
                hold_pool(13).then_inc(sem("scatter_held"), 1)
                for t in range(2):
                    pool.indirect_dma_start(x_sorted, bass.IndirectOffsetOnAxis(
                        ap=pos_i[par][:, 2 * k + t:2 * k + t + 1].bitcast(U32), axis=0), xs[par][:, t], None
                        ).then_inc(sem("scattered"), 16)

            bodies(pool, step)

            for k in range(2):
                scatter(NB - 1, 1, k)

            def load_rows(n):
                par = n % 2
                if n >= 3:
                    pool.wait_ge(sem("unitT_done"), 2 * (n - 1))
                if n > NJ:
                    c = n - NJ
                    pool.dma_start(xg[par][:], x1_v[:, 4 * c:4 * c + 4]).then_inc(sem(f"xg{par}_loaded"), 64)
                    return
                for t in range(4):
                    pool.indirect_dma_start(xg[par][:, t], None, x_sorted, bass.IndirectOffsetOnAxis(
                        ap=row_i[:, n - 1, t:t + 1].bitcast(U32), axis=0)).then_inc(sem(f"xg{par}_loaded"), 16)

            def load_weights(n, raw, table_, name):
                pool.wait_ge(sem(name + "_hi_done"), n)
                pool.wait_ge(sem(name + "_lo_done"), n)
                if n > NJ:
                    pool.dma_start(raw[:], table_[0:P]).then_inc(sem(name + "_loaded"), 16)
                else:
                    pool.indirect_dma_start(raw[:], None, table_, bass.IndirectOffsetOnAxis(
                        ap=wrow_i[:, n - 1:n].bitcast(U32), axis=0)).then_inc(sem(name + "_loaded"), 16)

            def gather_results(c):
                par = c % 2
                if c >= 2:
                    pool.wait_ge(sem("combine_step"), 8 * (c - 1))
                for k in range(2):
                    for t in range(4):
                        b, tt = divmod(4 * c + t, 2)
                        pool.indirect_dma_start(yg[par][:, k, t], None, y_sorted, bass.IndirectOffsetOnAxis(
                            ap=yrow_i[:, b, 2 * k + tt:2 * k + tt + 1].bitcast(U32), axis=0)
                            ).then_inc(sem(f"yg{par}_loaded"), 16)

            def inv_std(c):
                pool.wait_ge(sem("mv2_done"), 4 * c + 4)
                if c >= 1:
                    pool.wait_ge(sem("out_ready"), 4 * c)
                pool.tensor_scalar(vps2[:], mv2[:, :, 1], 1.0, LN_EPS, ALU.mult, ALU.add).then_inc(sem("vps2"), 1)
                pool.wait_ge(sem("vps2"), c + 1)
                pool.tensor_tensor(rs2[:], vps2[:], mhalf4[:], ALU.pow).then_inc(sem("rs2_done"), 1)
                pool.wait_ge(sem("rs2_done"), c + 1)
                pool.tensor_tensor(mr2[:], mv2[:, :, 0], rs2[:], ALU.mult).then_inc(sem("mr2_done"), 1)
                pool.wait_ge(sem("mr2_done"), c + 1)
                pool.tensor_scalar(nb2[:], mr2[:], -1.0, 0.0, ALU.mult, ALU.add).then_inc(sem("ln2_done"), 1)

            pool.wait_ge(sem("ln_done"), 2 * NB)
            pool.memset(mhalf4[:], -0.5).then_inc(sem("mhalf4_set"), 1)
            pool.wait_ge(sem("mhalf4_set"), 1)
            pool.wait_ge(sem("wrows_ready"), 1)
            for n in range(1, NJ + 2):
                load_weights(n, w13_raw, w13_all, "w13")
                if n == 1:
                    pool.wait_ge(sem("rows_ready"), 1)
                    pool.wait_ge(sem("scattered"), 64 * NB)
                    load_rows(1)
                load_rows(n + 1)
                load_weights(n, w2_raw, w2_all, "w2")
            load_rows(NJ + 3)
            pool.wait_ge(sem("yrows_ready"), 1)
            pool.wait_ge(sem("y_stored0"), 16 * (NJ // 2))
            pool.wait_ge(sem("y_stored1"), 16 * (NJ // 2 + 1))
            for c in range(NC):
                if c >= 2:
                    inv_std(c - 2)
                gather_results(c)
                if NJ + 4 + c < NU:
                    load_rows(NJ + 4 + c)
            inv_std(NC - 2)
            inv_std(NC - 1)


def kernel(**inputs):
    import numpy as np
    import concourse.bacc as bacc
    from concourse.bass_utils import run_bass_kernel_spmd

    g = {k: np.asarray(v) for k, v in inputs.items()}
    x = g["L0_attn_hidden_states"]

    def t(a):
        return np.ascontiguousarray(np.swapaxes(a, -1, -2))

    w13 = np.zeros((E + 1, P, W13), np.float32)
    w2t = np.zeros((E + 1, P, W2), np.float32)
    for e in range(E + 1):
        w1, w2, w3 = ((g["L0_ffn_sw1"], g["L0_ffn_sw2"], g["L0_ffn_sw3"]) if e == 0 else
                      (g["L0_ffn_ew1"][e - 1], g["L0_ffn_ew2"][e - 1], g["L0_ffn_ew3"][e - 1]))
        for k in range(2):
            w13[e, :, k * HF:(k + 1) * HF] = w1.T[k * P:(k + 1) * P]
            w13[e, :, W3_AT + k * HF:W3_AT + (k + 1) * HF] = w3.T[k * P:(k + 1) * P]
        for k, rows in enumerate(MT):
            w2t[e, :rows, k * D:(k + 1) * D] = w2.T[k * P:k * P + rows]
    table = np.zeros((P, T_COLS), np.float32)
    table[:, T_RANK:T_RANK + E] = np.arange(E, 0, -1)
    table[:, T_REGION:T_REGION + E] = np.arange(E) * REGION
    table[:, T_THR:T_THR + E] = np.arange(E) * C
    table[:, T_EIDX:T_EIDX + E] = np.arange(E)
    table[:, T_LTRI:T_LTRI + E * E] = np.tril(np.ones((E, E))).reshape(1, -1)
    table[:, T_J1:T_J1 + NJ] = np.arange(NJ) + 1
    table[:, T_TP:T_TP + 4] = np.arange(P)[:, None] + P * np.arange(4)
    table[:, T_P] = P + np.arange(P)
    mats = np.stack([np.triu(np.ones((P, P)), 1), np.ones((P, P))]).astype(np.float32)
    inv_freq = (1.0 / np.float32(10000.0) ** (np.arange(0, DR, 2, dtype=np.float32) / np.float32(DR))
                ).astype(np.float32)
    fr = np.outer(np.arange(S, dtype=np.float32), inv_freq).astype(np.float32)
    rope = np.stack([np.concatenate([np.cos(fr), np.cos(fr)], -1),
                     np.concatenate([-np.sin(fr), np.sin(fr)], -1)]).astype(np.float32)
    arrays = {
        "x_in": x, "xT_in": t(x),
        "waT_in": np.ascontiguousarray(np.concatenate([g["L0_attn_w_qa"], g["L0_attn_w_kva"]], 0).T),
        "wqb_in": g["L0_attn_w_qb"], "wqbT_in": t(g["L0_attn_w_qb"]), "wkvb_in": g["L0_attn_w_kvb"],
        "woT_in": t(g["L0_attn_w_o"]), "aln_in": g["L0_attn_q_a_ln_w"], "kvln_in": g["L0_attn_kv_a_ln_w"],
        "rope_in": rope, "wrT_in": t(g["L0_ffn_wr"]), "w13_in": w13.reshape(-1, W13), "w2_in": w2t.reshape(-1, W2),
        "table_in": table, "mats_in": mats,
    }
    nc = bacc.Bacc("TRN2", target_bir_lowering=False, num_devices=1)
    args = [nc.dram_tensor(k, a.shape, F32, kind="ExternalInput").ap() for k, a in arrays.items()]
    args.append(nc.dram_tensor("x1_scratch", x.shape, F32, kind="Internal").ap())
    args.append(nc.dram_tensor("x_sorted", (E * REGION, D), F32, kind="Internal").ap())
    args.append(nc.dram_tensor("y_sorted", (NJ * C, D), F32, kind="Internal").ap())
    args.append(nc.dram_tensor("out_dram", x.shape, F32, kind="ExternalOutput").ap())
    build(nc, *args)
    r = run_bass_kernel_spmd(nc, [arrays], core_ids=[0])
    return r.results[0]["out_dram"]
```
